# Optimizing a Trainium2 kernel written in Bass

```python
import numpy as np
import jax
import jax.numpy as jnp

def _softmax(x, axis=-1):
    return jax.nn.softmax(x, axis=axis)

def _gelu(x):
    return jax.nn.gelu(x, approximate=True)

def _silu(x):
    return jax.nn.silu(x)

def _sigmoid(x):
    return jax.nn.sigmoid(x)

def _layernorm(x, axis=-1, eps=1e-05):
    m = jnp.mean(x, axis=axis, keepdims=True)
    v = jnp.var(x, axis=axis, keepdims=True)
    return (x - m) / jnp.sqrt(v + eps)

def _scatter_add(tgt, idx, src, axis=0):
    return tgt.at[idx].add(src)

def _segment_sum(src, seg, n):
    return jax.ops.segment_sum(src, seg, n)
kernel_name = 'mk_early_fusion_d1_tok_img768_r4_c110a7'

def setup_inputs(seed: int=0):
    np.random.seed(seed)
    _w = jnp.asarray

    def _rec_inputs():
        import jax
        import jax.numpy as jnp
        _rk = jax.random.key(seed)
        x = -0.000356955 + 1 * jax.random.normal(jax.random.fold_in(_rk, 1), (64, 3, 224, 224), jnp.float32)
        txt = 8.44072e-05 + 0.997355 * jax.random.normal(jax.random.fold_in(_rk, 2), (64, 77, 192), jnp.float32)
        return (x, txt)
    x, txt = _rec_inputs()

    def _L0_tok_setup():
        import jax, jax.numpy as jnp
        import numpy as np
        P = 16

        def _patchify(x):
            B, C, H, Wd = x.shape
            Hp, Wp = (H // P, Wd // P)
            x = x.reshape(B, C, Hp, P, Wp, P)
            x = x.transpose(0, 2, 4, 1, 3, 5)
            return x.reshape(B, Hp * Wp, C * P * P)
        key = jax.random.key(seed)
        k1, k2, k3 = jax.random.split(key, 3)
        B, C, H, W_img = (128, 3, 224, 224)
        E = 192
        x = jax.random.normal(k1, (B, C, H, W_img), dtype=jnp.float32)
        W = jax.random.normal(k2, (C * P * P, E), dtype=jnp.float32) * (1.0 / np.sqrt(C * P * P))
        b = jnp.zeros((E,), dtype=jnp.float32)
        cls_token = jax.random.normal(k3, (1, 1, E), dtype=jnp.float32) * 0.02
        return {'x': x, 'W': W, 'b': b, 'cls_token': cls_token}
    _L0_tok_all = _L0_tok_setup()
    _L0_tok_in = {k: v for k, v in _L0_tok_all.items() if k in ('W', 'b', 'cls_token')}
    del _L0_tok_all

    def _L0_attn_setup():
        import jax, jax.numpy as jnp
        import numpy as np
        B, S, E, H = (1, 512, 192, 12)
        D = E // H
        EPS = 1.0
        N_IT = 3
        LN_EPS = 1e-12

        def _sinkhorn_plan(scores):
            C = -scores
            n = scores.shape[-1]
            log_mu = -jnp.log(jnp.asarray(n, scores.dtype))

            def M(u, v):
                return (-C + u[..., :, None] + v[..., None, :]) / EPS
            u = jnp.zeros(scores.shape[:-1], scores.dtype)
            v = jnp.zeros(scores.shape[:-1], scores.dtype)

            def step(carry, _):
                u, v = carry
                u = EPS * (log_mu - jax.scipy.special.logsumexp(M(u, v), axis=-1)) + u
                v = EPS * (log_mu - jax.scipy.special.logsumexp(M(u, v), axis=-2)) + v
                return ((u, v), None)
            (u, v), _ = jax.lax.scan(step, (u, v), None, length=N_IT)
            return jnp.exp(M(u, v))
        key = jax.random.key(seed)
        ks = jax.random.split(key, 9)
        s = 0.02
        return {'hidden_states': jax.random.normal(ks[0], (B, S, E), jnp.float32), 'Wq': jax.random.normal(ks[1], (E, E), jnp.float32) * s, 'bq': jnp.zeros((E,), jnp.float32), 'Wk': jax.random.normal(ks[2], (E, E), jnp.float32) * s, 'bk': jnp.zeros((E,), jnp.float32), 'Wv': jax.random.normal(ks[3], (E, E), jnp.float32) * s, 'bv': jnp.zeros((E,), jnp.float32), 'Wo': jax.random.normal(ks[4], (E, E), jnp.float32) * s, 'bo': jnp.zeros((E,), jnp.float32), 'ln_g': jnp.ones((E,), jnp.float32), 'ln_b': jnp.zeros((E,), jnp.float32)}
    _L0_attn_all = _L0_attn_setup()
    _L0_attn_in = {k: v for k, v in _L0_attn_all.items() if k in ('Wq', 'bq', 'Wk', 'bk', 'Wv', 'bv', 'Wo', 'bo', 'ln_g', 'ln_b')}
    del _L0_attn_all

    def _L0_ffn_setup():
        import math
        import jax, jax.numpy as jnp
        import numpy as np
        EMBED_CHOICES = [96, 144, 192]
        RATIO_CHOICES = [2, 3, 4]
        E_MAX = 192
        H_MAX = 768

        def new_gelu(x):
            c = math.sqrt(2.0 / math.pi)
            return 0.5 * x * (1.0 + jnp.tanh(c * (x + 0.044715 * x * x * x)))

        def _mixed_coeffs(alpha_e, alpha_r):
            h_idx = jnp.arange(H_MAX)
            d_idx = jnp.arange(E_MAX)
            C0 = jnp.zeros((H_MAX, E_MAX), jnp.float32)
            c0b = jnp.zeros((H_MAX,), jnp.float32)
            C1 = jnp.zeros((E_MAX, H_MAX), jnp.float32)
            c1b = jnp.zeros((E_MAX,), jnp.float32)
            for i, e in enumerate(EMBED_CHOICES):
                m_in = (d_idx < e).astype(jnp.float32)
                for j, r in enumerate(RATIO_CHOICES):
                    a = alpha_e[i] * alpha_r[j]
                    m_out = (h_idx < r * e).astype(jnp.float32)
                    C0 = C0 + a * (m_out[:, None] * m_in[None, :])
                    c0b = c0b + a * m_out
                    C1 = C1 + a * (m_in[:, None] * m_out[None, :])
                    c1b = c1b + a * m_in
            return (C0, c0b, C1, c1b)
        key = jax.random.key(seed)
        ks = jax.random.split(key, 6)
        x = jax.random.normal(ks[0], (8, 512, E_MAX), jnp.float32)
        w_fc = jax.random.normal(ks[1], (H_MAX, E_MAX), jnp.float32) * 0.02
        b_fc = jnp.zeros((H_MAX,), jnp.float32)
        w_proj = jax.random.normal(ks[2], (E_MAX, H_MAX), jnp.float32) * 0.02
        b_proj = jnp.zeros((E_MAX,), jnp.float32)
        alpha_e = jax.nn.softmax(jax.random.normal(ks[3], (3,), jnp.float32))
        alpha_r = jax.nn.softmax(jax.random.normal(ks[4], (3,), jnp.float32))
        return {'x': x, 'w_fc': w_fc, 'b_fc': b_fc, 'w_proj': w_proj, 'b_proj': b_proj, 'alpha_e': alpha_e, 'alpha_r': alpha_r}
    _L0_ffn_all = _L0_ffn_setup()
    _L0_ffn_in = {k: v for k, v in _L0_ffn_all.items() if k in ('w_fc', 'b_fc', 'w_proj', 'b_proj', 'alpha_e', 'alpha_r')}
    del _L0_ffn_all
    return {'x': x, 'txt': txt, 'L0_tok_W': _L0_tok_in['W'], 'L0_tok_b': _L0_tok_in['b'], 'L0_tok_cls_token': _L0_tok_in['cls_token'], 'L0_attn_Wq': _L0_attn_in['Wq'], 'L0_attn_bq': _L0_attn_in['bq'], 'L0_attn_Wk': _L0_attn_in['Wk'], 'L0_attn_bk': _L0_attn_in['bk'], 'L0_attn_Wv': _L0_attn_in['Wv'], 'L0_attn_bv': _L0_attn_in['bv'], 'L0_attn_Wo': _L0_attn_in['Wo'], 'L0_attn_bo': _L0_attn_in['bo'], 'L0_attn_ln_g': _L0_attn_in['ln_g'], 'L0_attn_ln_b': _L0_attn_in['ln_b'], 'L0_ffn_w_fc': _L0_ffn_in['w_fc'], 'L0_ffn_b_fc': _L0_ffn_in['b_fc'], 'L0_ffn_w_proj': _L0_ffn_in['w_proj'], 'L0_ffn_b_proj': _L0_ffn_in['b_proj'], 'L0_ffn_alpha_e': _L0_ffn_in['alpha_e'], 'L0_ffn_alpha_r': _L0_ffn_in['alpha_r']}

def reference(x, txt, L0_tok_W, L0_tok_b, L0_tok_cls_token, L0_attn_Wq, L0_attn_bq, L0_attn_Wk, L0_attn_bk, L0_attn_Wv, L0_attn_bv, L0_attn_Wo, L0_attn_bo, L0_attn_ln_g, L0_attn_ln_b, L0_ffn_w_fc, L0_ffn_b_fc, L0_ffn_w_proj, L0_ffn_b_proj, L0_ffn_alpha_e, L0_ffn_alpha_r):
    import jax
    import jax.numpy as jnp

    def _L0_tok_ref(x, W, b, cls_token):
        import jax, jax.numpy as jnp
        import numpy as np
        P = 16

        def _patchify(x):
            B, C, H, Wd = x.shape
            Hp, Wp = (H // P, Wd // P)
            x = x.reshape(B, C, Hp, P, Wp, P)
            x = x.transpose(0, 2, 4, 1, 3, 5)
            return x.reshape(B, Hp * Wp, C * P * P)
        B = x.shape[0]
        patches = _patchify(x)
        emb = jnp.einsum('blk,ke->ble', patches, W) + b
        cls = jnp.broadcast_to(cls_token, (B, 1, cls_token.shape[-1]))
        out = jnp.concatenate([cls, emb], axis=1)
        return out

    def _L0_attn_ref(hidden_states, Wq, bq, Wk, bk, Wv, bv, Wo, bo, ln_g, ln_b):
        import jax, jax.numpy as jnp
        import numpy as np
        B, S, E, H = (1, 512, 192, 12)
        D = E // H
        EPS = 1.0
        N_IT = 3
        LN_EPS = 1e-12

        def _sinkhorn_plan(scores):
            C = -scores
            n = scores.shape[-1]
            log_mu = -jnp.log(jnp.asarray(n, scores.dtype))

            def M(u, v):
                return (-C + u[..., :, None] + v[..., None, :]) / EPS
            u = jnp.zeros(scores.shape[:-1], scores.dtype)
            v = jnp.zeros(scores.shape[:-1], scores.dtype)

            def step(carry, _):
                u, v = carry
                u = EPS * (log_mu - jax.scipy.special.logsumexp(M(u, v), axis=-1)) + u
                v = EPS * (log_mu - jax.scipy.special.logsumexp(M(u, v), axis=-2)) + v
                return ((u, v), None)
            (u, v), _ = jax.lax.scan(step, (u, v), None, length=N_IT)
            return jnp.exp(M(u, v))
        b, s, e = hidden_states.shape

        def heads(x):
            return x.reshape(b, s, H, D).transpose(0, 2, 1, 3)
        q = heads(hidden_states @ Wq + bq)
        k = heads(hidden_states @ Wk + bk)
        v = heads(hidden_states @ Wv + bv)
        scores = jnp.einsum('bhsd,bhtd->bhst', q, k) / np.sqrt(D).astype(np.float32)
        attn = _sinkhorn_plan(scores) * jnp.asarray(s, scores.dtype)
        ctx = jnp.einsum('bhst,bhtd->bhsd', attn, v)
        ctx = ctx.transpose(0, 2, 1, 3).reshape(b, s, e)
        y = ctx @ Wo + bo + hidden_states
        mu = jnp.mean(y, axis=-1, keepdims=True)
        var = jnp.mean(jnp.square(y - mu), axis=-1, keepdims=True)
        return ln_g * (y - mu) / jnp.sqrt(var + LN_EPS) + ln_b

    def _L0_ffn_ref(x, w_fc, b_fc, w_proj, b_proj, alpha_e, alpha_r):
        import math
        import jax, jax.numpy as jnp
        import numpy as np
        EMBED_CHOICES = [96, 144, 192]
        RATIO_CHOICES = [2, 3, 4]
        E_MAX = 192
        H_MAX = 768

        def new_gelu(x):
            c = math.sqrt(2.0 / math.pi)
            return 0.5 * x * (1.0 + jnp.tanh(c * (x + 0.044715 * x * x * x)))

        def _mixed_coeffs(alpha_e, alpha_r):
            h_idx = jnp.arange(H_MAX)
            d_idx = jnp.arange(E_MAX)
            C0 = jnp.zeros((H_MAX, E_MAX), jnp.float32)
            c0b = jnp.zeros((H_MAX,), jnp.float32)
            C1 = jnp.zeros((E_MAX, H_MAX), jnp.float32)
            c1b = jnp.zeros((E_MAX,), jnp.float32)
            for i, e in enumerate(EMBED_CHOICES):
                m_in = (d_idx < e).astype(jnp.float32)
                for j, r in enumerate(RATIO_CHOICES):
                    a = alpha_e[i] * alpha_r[j]
                    m_out = (h_idx < r * e).astype(jnp.float32)
                    C0 = C0 + a * (m_out[:, None] * m_in[None, :])
                    c0b = c0b + a * m_out
                    C1 = C1 + a * (m_in[:, None] * m_out[None, :])
                    c1b = c1b + a * m_in
            return (C0, c0b, C1, c1b)
        C0, c0b, C1, c1b = _mixed_coeffs(alpha_e, alpha_r)
        W0 = w_fc * C0
        b0 = b_fc * c0b
        h = jnp.einsum('bte,he->bth', x, W0) + b0
        h = new_gelu(h)
        W1 = w_proj * C1
        b1 = b_proj * c1b
        out = jnp.einsum('bth,eh->bte', h, W1) + b1
        return out
    h = _L0_tok_ref(x, L0_tok_W, L0_tok_b, L0_tok_cls_token)
    h = jnp.concatenate([h, txt], axis=1)
    h = h + _L0_attn_ref(_layernorm(h, axis=-1), L0_attn_Wq, L0_attn_bq, L0_attn_Wk, L0_attn_bk, L0_attn_Wv, L0_attn_bv, L0_attn_Wo, L0_attn_bo, L0_attn_ln_g, L0_attn_ln_b)
    h = h + _L0_ffn_ref(_layernorm(h, axis=-1), L0_ffn_w_fc, L0_ffn_b_fc, L0_ffn_w_proj, L0_ffn_b_proj, L0_ffn_alpha_e, L0_ffn_alpha_r)
    return h

_drawn_inputs = setup_inputs


def setup_inputs(seed=0):
    import zlib

    import numpy as np

    out = dict(_drawn_inputs(seed))
    spreads = {'L0_tok_b': (0.0, 0.1),
     'L0_attn_bq': (0.0, 2.0),
     'L0_attn_bk': (0.0, 2.0),
     'L0_attn_bv': (0.0, 0.544),
     'L0_attn_bo': (0.0, 0.8),
     'L0_attn_ln_g': (1.0, 0.2),
     'L0_attn_ln_b': (0.0, 0.481),
     'L0_ffn_b_fc': (0.0, 0.8),
     'L0_ffn_b_proj': (0.0, 0.552)}
    factors = {'L0_attn_Wq': 8.0,
     'L0_attn_Wk': 8.0,
     'L0_attn_Wv': 8.0,
     'L0_attn_Wo': 4.294,
     'L0_ffn_alpha_e': 3.532,
     'L0_ffn_alpha_r': 8.0,
     'L0_tok_cls_token': 3.232}
    for name, (base, spread) in spreads.items():
        noise = np.random.default_rng([zlib.crc32(name.encode()), seed]).standard_normal(out[name].shape)
        drawn = base * np.exp(spread * noise) if base else spread * noise
        out[name] = jnp.asarray(drawn.astype(out[name].dtype))
    for name, factor in factors.items():
        out[name] = (out[name] * factor).astype(out[name].dtype)
    return out
```

```python
from contextlib import ExitStack

import concourse.bass as bass
from concourse import mybir

ALU = mybir.AluOpType
ACT = mybir.ActivationFunctionType
AX_X = mybir.AxisListType.X
F32 = mybir.dt.float32
BF16 = mybir.dt.bfloat16

P = 128
E = 192
H = 12
D = E // H
S = 274
NPATCH = 196
NTXT = 77
KC = 768 // P
REST = S - 2 * P
SP = 2 * P + 32
CLS_ROW = NPATCH - P
HALF = E // 2
HH = H // 2
GROUPS = H // 4
TILES = 9 * GROUPS
HID = 768
HC = HID // P
PARTS = 3
Q_BLOCKS = (0, 0, 1, 1, 0, 2)
K_BLOCKS = (0, 1, 0, 1, 2, 0)
NBLK = len(Q_BLOCKS)
L_ROW = NBLK * D
M_ROW = L_ROW + PARTS
STACK = M_ROW + PARTS
PREP_STEPS = 46
NEG = -1.0e30
LN_EPS, ATTN_EPS = 1e-5, 1e-12
EMBED_CHOICES = (96, 144, 192)
RATIO_CHOICES = (2, 3, 4)

JOBS = (
    ["H4_0", "H4_1", "T4_0", "H4_2", "T4_1", "H5_0", "T4_2", "H5_1", "T5_0", "H5_2", "T5_1",
     "H6_0", "T5_2", "H6_1", "T6_0", "H6_2", "T6_1", "C_0", "T6_2", "C_1", "C_2"]
    + ["L"] + ["W_0", "W_1", "W_2", "X_0", "X_1"] + [f"G_{c}" for c in range(HC)] + ["O_0", "O_1", "O_2"]
    + ["E_0", "E_1", "M", "N_0", "N_1", "Q_0", "Q_1", "K_0", "K_1", "V_0", "V_1", "V_2"]
)
NBANK = 4
STAGE = {n: "mid" if n in ("L", "M") else "front" if n[0] in "ENQKV" else "back" for n in JOBS}
BANK = {n: i % NBANK for i, n in enumerate(JOBS)}
RING = 4
RING_USES = [len(range(r, 3 * TILES, RING)) for r in range(RING)]

LINKS = {"front": 2 + 4 * 3, "mid": 10, "back": 14}


def tile_of(k):
    g, i = divmod(k, 9)
    return (g, None, 2) if i == 8 else (g, 4 * g + i // 2, i % 2)


def column_of(k):
    g, h, c = tile_of(k)
    return 2 * H + g if h is None else c * H + h


class Pass:

    def __init__(self, images, banks_before):
        self.images = images
        self.banks_before = banks_before
        self.back, self.mid, self.front = images["back"], images["mid"], images["front"]

    def active(self, job):
        return self.images[STAGE[job]] is not None

    def uses_before(self, job):
        mine = [n for n in JOBS if self.active(n) and BANK[n] == BANK[job]]
        return self.banks_before[BANK[job]] + mine.index(job)

    def uses_before_pass(self, job):
        later = [n for n in JOBS[JOBS.index(job) + 1:] if BANK[n] == BANK[job] and STAGE[n] == "front"]
        return self.banks_before[BANK[job]] - len(later)

    def uses(self):
        return [sum(self.active(n) and BANK[n] == r for n in JOBS) for r in range(NBANK)]


def images_of(it, B):
    return {"back": it if 0 <= it < B else None, "mid": it + 1 if 0 <= it + 1 < B else None,
            "front": it + 2 if 0 <= it + 2 < B else None}


def run_passes(engine, B, one_pass):
    before = [0] * NBANK

    def fixed(it):
        nonlocal before
        p = Pass(images_of(it, B), list(before))
        one_pass(p)
        before = [a + b for a, b in zip(before, p.uses())]

    fixed(-2)
    fixed(-1)
    full = Pass({"back": 0, "mid": 1, "front": 2}, before).uses()
    with engine.Fori(0, B - 2) as it:
        one_pass(Pass({"back": it, "mid": it + 1, "front": it + 2},
                      [it * n + a for n, a in zip(full, before)]))
    before = [a + (B - 2) * n for a, n in zip(before, full)]
    fixed(B - 2)
    fixed(B - 1)


def early_fusion_kernel(nc, x, txt, tok_w, tok_b, cls, wq, wk, wv, wo, bq, bk, bv, bo, ln_g, ln_b,
                        w_fc, b_fc, w_proj, b_proj, alpha_e, alpha_r, out):
    B = x.shape[0]
    with ExitStack() as ctx:
        def sb(name, shape, dt=F32):
            return ctx.enter_context(nc.sbuf_tensor(name, shape, dt))

        def sem(name):
            return ctx.enter_context(nc.semaphore(name))

        ident = sb("ident", [P, P])
        ident_bf = sb("ident_bf", [P, P], BF16)
        mask12 = sb("mask12", [P, 12])
        mask_rest = sb("mask_rest", [P, 1])
        pad_one = sb("pad_one", [P, 1])
        pad_neg = sb("pad_neg", [P, 1])
        minus_half = sb("minus_half", [P, 3])
        tok_w_sb = sb("tok_w_sb", [P, KC, E])
        wq_sb = sb("wq_sb", [HALF, 2, 2, HALF])
        wk_sb = sb("wk_sb", [HALF, 2, 2, HALF])
        wv_sb = sb("wv_sb", [HALF, 2, E])
        wo_sb = sb("wo_sb", [P, GROUPS, E])
        w0_sb = sb("w0_sb", [HALF, 2, HID])
        w1_sb = sb("w1_sb", [P, HC, E])
        bq_sb = sb("bq_sb", [HALF, 2])
        bk_sb = sb("bk_sb", [HALF, 2])
        tok_b_sb = sb("tok_b_sb", [P, E])
        bv_sb = sb("bv_sb", [P, E])
        bo_sb = sb("bo_sb", [P, E])
        ln_g_sb = sb("ln_g_sb", [P, E])
        ln_b_sb = sb("ln_b_sb", [P, E])
        b1_sb = sb("b1_sb", [P, E])
        b0_sb = sb("b0_sb", [P, HC])
        alpha_sb = sb("alpha_sb", [P, 6])
        pair = sb("pair", [P, 9])
        below = sb("below", [P, 9, HC])
        coef = sb("coef", [P, 3, HC])
        coef_row = sb("coef_row", [HALF, 2, HID])
        coef_out = sb("coef_out", [P, 3])
        fence = sb("fence", [P, 1])

        x_sb = sb("x_sb", [P, KC, NPATCH])
        h_sb = sb("h_sb", [P, 3, E])
        hn_sb = sb("hn_sb", [P, 3, E])
        hnT = sb("hnT", [HALF, 2, SP])
        qk_f = sb("qk_f", [HALF, 4, SP])
        qk_r = sb("qk_r", [HALF, 4, SP])
        qk_parts = sb("qk_parts", [HALF, 4, PARTS, SP], BF16)
        v_sb = sb("v_sb", [P, 3, E])
        stats_f = sb("stats_f", [P, 3, 6])
        mv_f = sb("mv_f", [P, 3, 2])
        rstd_f = sb("rstd_f", [P, 3])
        q_stack = sb("q_stack", [STACK, H, SP], BF16)
        k_stack = sb("k_stack", [STACK, H, SP], BF16)
        neg_r = sb("neg_r", [P, TILES])
        neg_c = sb("neg_c", [P, TILES])
        rho = sb("rho", [P, TILES])
        kappa = sb("kappa", [P, TILES])
        sigma = sb("sigma", [P, TILES])
        ln_sum = sb("ln_sum", [P, TILES])
        log_f = sb("log_f", [P, TILES])
        log_r = sb("log_r", [P, TILES])
        log_parts = sb("log_parts", [P, PARTS * TILES], BF16)
        log_rows = sb("log_rows", [PARTS * H, 2 * P], BF16)
        log_rest = sb("log_rest", [PARTS * GROUPS, P], BF16)
        junk = sb("junk", [P, RING, S], BF16)
        G = sb("G", [P, TILES, S])
        PL = sb("PL", [P, TILES, S])
        rest_tmp = sb("rest_tmp", [P, GROUPS])
        sigma_rest = sb("sigma_rest", [P, GROUPS])
        inv_kappa = sb("inv_kappa", [P, GROUPS, 12])
        w_a = sb("w_a", [P, GROUPS, 12])
        w_b = sb("w_b", [P, GROUPS, 12])
        w_a2 = sb("w_a2", [P, GROUPS, 12])
        w_b2 = sb("w_b2", [P, GROUPS, 12])
        recip12 = sb("recip12", [P, GROUPS, 12])
        sums = sb("sums", [P, GROUPS, SP])
        ln_row = sb("ln_row", [P, GROUPS, S])
        a_row = sb("a_row", [P, GROUPS, SP])
        v_cur = sb("v_cur", [P, 3, E])
        v_w = sb("v_w", [P, GROUPS, 12, 32])
        ctxT = sb("ctxT", [P, GROUPS, S])
        hbo_cur = sb("hbo_cur", [P, 3, E])
        hlb_cur = sb("hlb_cur", [P, 3, E])
        y_sb = sb("y_sb", [P, 3, E])
        h2_sb = sb("h2_sb", [P, 3, E])
        h2n_sb = sb("h2n_sb", [P, 3, E])
        h2b_sb = sb("h2b_sb", [P, 3, E])
        stats_b = sb("stats_b", [P, 3, 6])
        mv_b = sb("mv_b", [P, 3, 2])
        rstd_b = sb("rstd_b", [P, 3])
        stats_c = sb("stats_c", [P, 3, 6])
        mv_c = sb("mv_c", [P, 3, 2])
        rstd_c = sb("rstd_c", [P, 3])
        h2T = sb("h2T", [HALF, 2, S])
        gT = sb("gT", [P, HC, S])
        out_sb = sb("out_sb", [P, 3, E])

        score = [ctx.enter_context(nc.psum_tensor(f"score{r}", [P, 512], F32)) for r in range(RING)]
        work = [ctx.enter_context(nc.psum_tensor(f"work{r}", [P, 512], F32)) for r in range(NBANK)]

        weights_in = sem("weights_in")
        pool_prep = sem("pool_prep")
        prep_step = sem("prep_step")
        x_in = sem("x_in")
        txt_in = sem("txt_in")
        score_full = [sem(f"score_full{r}") for r in range(RING)]
        score_free = [sem(f"score_free{r}") for r in range(RING)]
        work_full = [sem(f"work_full{r}") for r in range(NBANK)]
        work_free = [sem(f"work_free{r}") for r in range(NBANK)]
        max_ready = sem("max_ready")
        ln_ready = sem("ln_ready")
        log_ready = sem("log_ready")
        log_stacked = sem("log_stacked")
        parts_ready = sem("parts_ready")
        stacked = sem("stacked")
        var_ready = {s: sem(f"var_ready_{s}") for s in "fbc"}
        rstd_ready = {s: sem(f"rstd_ready_{s}") for s in "fbc"}
        hn_ready = sem("hn_ready")
        kappa_ready = sem("kappa_ready")
        v_ready = sem("v_ready")
        cur_ready = sem("cur_ready")
        first_weights = sem("first_weights")
        half_weights = sem("half_weights")
        a_row_ready = sem("a_row_ready")
        v_weighted = sem("v_weighted")
        h2_ready = sem("h2_ready")
        h2n_ready = sem("h2n_ready")
        h2b_ready = sem("h2b_ready")
        out_stored = sem("out_stored")
        vector_step = {s: sem(f"vector_step_{s}") for s in LINKS}

        ROWS = (P, P, REST)
        WIDE = ((slice(0, 2), P), (slice(2, 3), REST))

        def spread(t, rows, n):
            return t[0:rows, :].unsqueeze(1).to_broadcast([rows, n, E])

        def wait(engine, semaphore, value):
            if not (isinstance(value, int) and value == 0):
                engine.wait_ge(semaphore, value)

        def wait_full(engine, p, job):
            engine.wait_ge(work_full[BANK[job]], p.uses_before(job) + 1)
            return work[BANK[job]]

        def wait_emptied(engine, p, job):
            engine.wait_ge(work_free[BANK[job]], p.uses_before(job) + 1)

        def wait_exp(engine, image, slot):
            engine.wait_ge(score_free[slot % RING], image * RING_USES[slot % RING] + slot // RING + 1)

        def wait_scores(engine, image, slot):
            engine.wait_ge(score_full[slot % RING], image * RING_USES[slot % RING] + slot // RING + 1)

        OUT_FREE = 1
        WEIGHT_DMAS = 9 + 6 + 3 + 4
        POOL_PREPS = 25

        block = ctx.enter_context(nc.Block())

        @block.sync
        def _(sp):
            for dst, src in ((tok_w_sb, tok_w), (wq_sb, wq), (wk_sb, wk), (wv_sb, wv), (w0_sb, w_fc),
                             (w1_sb, w_proj), (bq_sb, bq), (bk_sb, bk), (b0_sb, b_fc)):
                sp.dma_start(dst[:], src).then_inc(weights_in, 16)
            for dst, src in ((tok_b_sb, tok_b), (bv_sb, bv), (bo_sb, bo), (ln_g_sb, ln_g),
                             (ln_b_sb, ln_b), (b1_sb, b_proj)):
                sp.dma_start(dst[:], src.partition_broadcast(P)).then_inc(weights_in, 16)
            sp.dma_start(alpha_sb[:, 0:3], alpha_e.partition_broadcast(P)).then_inc(weights_in, 16)
            sp.dma_start(alpha_sb[:, 3:6], alpha_r.partition_broadcast(P)).then_inc(weights_in, 16)
            sp.dma_start(h_sb[CLS_ROW:CLS_ROW + 1, 1, :], cls).then_inc(weights_in, 16)
            sp.wait_ge(pool_prep, 1)
            for j in range(4):
                sp.dma_start(wo_sb[32 * j:32 * j + D, :, :], wo[j]).then_inc(weights_in, 16)
            sp.wait_ge(prep_step, PREP_STEPS)

            def store_logs(p, job, n, stack, row):
                wait_emptied(sp, p, job)
                sp.dma_start(stack[row:row + PARTS, :, 0:2 * P], log_rows[:]).then_inc(log_stacked, 16)
                sp.dma_start(stack[row:row + PARTS, :, 2 * P:SP], log_rest[:]).then_inc(log_stacked, 16)

            def one_pass(p):
                if p.front is not None:
                    wait(sp, work_full[BANK["E_1"]], p.uses_before_pass("E_1") if p.mid is not None else 0)
                    sp.dma_start(x_sb[:], x[p.front]).then_inc(x_in, 16)
                if p.mid is not None:
                    store_logs(p, "L", 0, q_stack, L_ROW)
                if p.front is not None:
                    if p.mid is not None:
                        sp.wait_ge(cur_ready, 5 * p.mid + 5)
                    sp.dma_start(h_sb[CLS_ROW + 1:P, 1, :],
                                 txt[p.front, 0:P - CLS_ROW - 1, :]).then_inc(txt_in, 16)
                    sp.dma_start(h_sb[0:REST, 2, :],
                                 txt[p.front, P - CLS_ROW - 1:NTXT, :]).then_inc(txt_in, 16)
                if p.back is not None:
                    wait_emptied(sp, p, "O_2")
                    sp.dma_start(out[p.back, 0:2 * P, :].rearrange("(c p) e -> p c e", p=P),
                                 out_sb[:, 0:2, :]).then_inc(out_stored, 16)
                    sp.dma_start(out[p.back, 2 * P:S, :], out_sb[0:REST, 2, :]).then_inc(out_stored, 16)
                if p.mid is not None:
                    store_logs(p, "M", 1, k_stack, M_ROW)
                if p.front is not None:
                    if p.mid is not None:
                        wait_scores(sp, p.mid, 3 * TILES - 1)
                    for t, (stack, blocks) in enumerate(((q_stack, Q_BLOCKS), (k_stack, K_BLOCKS))):
                        for m in range(2):
                            sp.wait_ge(parts_ready, 4 * p.front + 2 * t + m + 1)
                            for i, part in enumerate(blocks):
                                sp.dma_start(stack[D * i:D * i + D, HH * m:HH * m + HH, :],
                                             qk_parts[:, 2 * t + m, part, :]).then_inc(stacked, 16)

            run_passes(sp, B, one_pass)
            sp.wait_ge(out_stored, 32 * B + OUT_FREE)

        @block.gpsimd
        def _(pool):
            count = [0]

            def prep(ins):
                count[0] += 1
                ins.then_inc(pool_prep, 1)

            def after():
                pool.wait_ge(pool_prep, count[0])

            prep(pool.memset(wo_sb[:], 0.0))
            prep(pool.memset(ident[:], 0.0))
            prep(pool.memset(mask12[:], 1.0))
            prep(pool.memset(below[:], 1.0))
            prep(pool.memset(minus_half[:], -0.5))
            after()
            prep(pool.affine_select(out=ident[:], in_=ident[:], compare_op=ALU.not_equal, fill=1.0,
                                    base=0, pattern=[[-1, P]], channel_multiplier=1))
            prep(pool.affine_select(out=mask12[:, 8:12], in_=mask12[:, 8:12], compare_op=ALU.is_ge,
                                    fill=0.0, base=0, pattern=[[-32, 4]], channel_multiplier=1))
            after()
            prep(pool.affine_select(out=mask12[:, 8:12], in_=mask12[:, 8:12], compare_op=ALU.is_ge,
                                    fill=0.0, base=REST - 1, pattern=[[32, 4]], channel_multiplier=-1))
            for i, e in enumerate(EMBED_CHOICES):
                for j, r in enumerate(RATIO_CHOICES):
                    m = below[:, 3 * i + j, :]
                    prep(pool.affine_select(out=m, in_=m, compare_op=ALU.is_ge, fill=0.0,
                                            base=r * e - 1, pattern=[[-P, HC]], channel_multiplier=-1))
            for t in (hnT, qk_parts, v_w):
                prep(pool.memset(t[:], 0.0))
            for t in (sums, a_row, mv_f, mv_b, mv_c):
                prep(pool.memset(t[:], 1.0))
            assert count[0] == POOL_PREPS, count[0]

            def rstd(which, mv, out_, n):
                pool.wait_ge(var_ready[which], n + 1)
                nc.gpsimd.tensor_tensor(out_[:], mv[:, :, 1], minus_half[:], ALU.pow)\
                    .then_inc(rstd_ready[which], 1)

            def one_pass(p):
                if p.back is not None:
                    rstd("b", mv_b, rstd_b, p.back)
                    pool.wait_ge(h2_ready, p.back + 1)
                    for c, rows in WIDE:
                        nc.gpsimd.tensor_tensor(h2b_sb[0:rows, c, :], h2_sb[0:rows, c, :],
                                                spread(b1_sb, rows, c.stop - c.start),
                                                ALU.add).then_inc(h2b_ready, 1)
                    rstd("c", mv_c, rstd_c, p.back)
                if p.mid is not None:
                    if p.back is not None:
                        pool.wait_ge(v_weighted, 3 * p.back + 3)
                    pool.wait_ge(v_ready, p.mid + 1)
                    for dst, src, bias in ((hbo_cur, hn_sb, bo_sb), (hlb_cur, h_sb, ln_b_sb)):
                        for c, rows in WIDE:
                            nc.gpsimd.tensor_tensor(dst[0:rows, c, :], src[0:rows, c, :],
                                                    spread(bias, rows, c.stop - c.start),
                                                    ALU.add).then_inc(cur_ready, 1)
                    nc.gpsimd.tensor_copy(v_cur[:], v_sb[:]).then_inc(cur_ready, 1)
                if p.front is not None:
                    rstd("f", mv_f, rstd_f, p.front)

            pool.wait_ge(weights_in, 16 * WEIGHT_DMAS)
            pool.wait_ge(prep_step, PREP_STEPS)
            run_passes(pool, B, one_pass)

        @block.tensor
        def _(pe):
            def work_bank(p, job):
                wait(pe, work_free[BANK[job]], p.uses_before(job))
                return work[BANK[job]]

            def done(job, last):
                last.then_inc(work_full[BANK[job]], 1)

            def score_tiles(p, which, lo, hi):
                if p.mid is None:
                    return
                for k in range(lo, hi):
                    if k == 0 and which == 0:
                        pe.wait_ge(stacked, 16 * 4 * NBLK * (p.mid + 1))
                    elif k == 0:
                        pe.wait_ge(log_stacked, 32 * (2 * p.mid + which))
                    slot = TILES * which + k
                    r = slot % RING
                    wait(pe, score_free[r], p.mid * RING_USES[r] + slot // RING)
                    rows = (L_ROW, M_ROW, STACK)[which]
                    still, move = (k_stack, q_stack) if which == 1 else (q_stack, k_stack)
                    g, h, c = tile_of(k)
                    if h is None:
                        for j in range(4):
                            last = nc.tensor.matmul(score[r][32 * j:32 * j + 32, 0:S],
                                                    still[0:rows, 4 * g + j, 2 * P:SP],
                                                    move[0:rows, 4 * g + j, 0:S], start=True, stop=True)
                    else:
                        last = nc.tensor.matmul(score[r][:, 0:S], still[0:rows, h, P * c:P * c + P],
                                                move[0:rows, h, 0:S], start=True, stop=True)
                    last.then_inc(score_full[r], 1)

            def four_heads(p, job, g, matrix, weights):
                bank = work_bank(p, job)
                for i in range(12):
                    c, j = divmod(i, 4)
                    k = 9 * g + (8 if c == 2 else 2 * j + c)
                    last = nc.tensor.matmul(bank[32 * j:32 * j + 32, 0:S], weights(i),
                                            matrix[:, k, :], start=(c == 0), stop=(c == 2))
                done(job, last)

            def half_sum(p, job, g, matrix, weights):
                four_heads(p, job, g, matrix,
                           lambda i: weights[:, g, i:i + 1].to_broadcast([P, 32]))

            def turn(p, job, g, rows):
                bank = work_bank(p, job)
                for c in range(2):
                    nc.tensor.transpose(bank[:, P * c:P * c + P], rows[:, g, P * c:P * c + P], ident[:])
                for j in range(4):
                    last = nc.tensor.matmul(bank[32 * j:32 * j + 32, 2 * P:3 * P:32],
                                            rows[:, g, 2 * P:SP], ident[:, 0:P:32], start=True, stop=True)
                done(job, last)

            def h4(p, g):
                if p.back is not None:
                    pe.wait_ge(first_weights, 3 * p.back + g + 1)
                    half_sum(p, f"H4_{g}", g, PL, w_a)

            def t4(p, g):
                if p.back is not None:
                    wait_emptied(pe, p, f"H4_{g}")
                    turn(p, f"T4_{g}", g, sums)

            def h5(p, g):
                if p.back is not None:
                    pe.wait_ge(half_weights, 3 * p.back + g + 1)
                    half_sum(p, f"H5_{g}", g, G, w_b)

            def t5(p, g):
                if p.back is not None:
                    pe.wait_ge(a_row_ready, 3 * p.back + g + 1)
                    turn(p, f"T5_{g}", g, a_row)

            def h6(p, g):
                if p.back is not None:
                    wait_emptied(pe, p, f"T5_{g}")
                    half_sum(p, f"H6_{g}", g, PL, w_a2)

            def t6(p, g):
                if p.back is not None:
                    wait_emptied(pe, p, f"H6_{g}")
                    turn(p, f"T6_{g}", g, sums)

            def context(p, g):
                if p.back is not None:
                    pe.wait_ge(v_weighted, 3 * p.back + g + 1)
                    four_heads(p, f"C_{g}", g, G, lambda i: v_w[:, g, i, :])

            def turn_logs(p, job, n):
                if p.mid is None:
                    return
                pe.wait_ge(log_ready, 2 * p.mid + n + 1)
                bank = work_bank(p, job)[:, :].bitcast(BF16)
                n = PARTS * H
                nc.tensor.transpose(bank[0:PARTS * GROUPS, 2 * P:3 * P],
                                    log_parts[:, 2 * n:PARTS * TILES], ident_bf[:])
                for c in range(2):
                    last = nc.tensor.transpose(bank[0:n, P * c:P * c + P],
                                               log_parts[:, n * c:n * c + n], ident_bf[:])
                done(job, last)

            def out_proj(p):
                if p.back is None:
                    return
                for g in range(GROUPS):
                    wait_emptied(pe, p, f"C_{g}")
                for t in range(3):
                    job = f"W_{t}"
                    bank = work_bank(p, job)
                    for g in range(GROUPS):
                        last = nc.tensor.matmul(bank[0:ROWS[t], 0:E], ctxT[:, g, P * t:P * t + ROWS[t]],
                                                wo_sb[:, g, :], start=(g == 0), stop=(g == GROUPS - 1))
                    done(job, last)

            def turn_tokens(p, job, half, src):
                bank = work_bank(p, job)
                for t in range(3):
                    last = nc.tensor.transpose(bank[0:HALF, P * t:P * t + ROWS[t]],
                                               src[0:ROWS[t], t, HALF * half:HALF * half + HALF],
                                               ident[0:ROWS[t], 0:ROWS[t]])
                done(job, last)

            def turn_h2(p):
                if p.back is not None:
                    pe.wait_ge(h2n_ready, p.back + 1)
                    for half in range(2):
                        turn_tokens(p, f"X_{half}", half, h2n_sb)

            def ffn_up(p, c):
                if p.back is None:
                    return
                if c == 0:
                    wait_emptied(pe, p, "X_0")
                    wait_emptied(pe, p, "X_1")
                job = f"G_{c}"
                bank = work_bank(p, job)
                for half in range(2):
                    last = nc.tensor.matmul(bank[:, 0:S], w0_sb[:, half, P * c:P * c + P],
                                            h2T[:, half, :], start=(half == 0), stop=(half == 1))
                done(job, last)

            def ffn_down(p, t):
                if p.back is None:
                    return
                if t == 0:
                    wait_emptied(pe, p, f"G_{HC - 1}")
                job = f"O_{t}"
                bank = work_bank(p, job)
                for c in range(HC):
                    last = nc.tensor.matmul(bank[0:ROWS[t], 0:E], gT[:, c, P * t:P * t + ROWS[t]],
                                            w1_sb[:, c, :], start=(c == 0), stop=(c == HC - 1))
                done(job, last)

            def embed(p, t):
                if p.front is None:
                    return
                if t == 0:
                    pe.wait_ge(x_in, 16 * (p.front + 1))
                job = f"E_{t}"
                bank = work_bank(p, job)
                rows = (P, NPATCH - P)[t]
                for c in range(KC):
                    last = nc.tensor.matmul(bank[0:rows, 0:E], x_sb[:, c, P * t:P * t + rows],
                                            tok_w_sb[:, c, :], start=(c == 0), stop=(c == KC - 1))
                done(job, last)

            def turn_hn(p):
                if p.front is not None:
                    pe.wait_ge(hn_ready, p.front + 1)
                    for half in range(2):
                        turn_tokens(p, f"N_{half}", half, hn_sb)

            def project(p, name, m, w):
                if p.front is None:
                    return
                if name == "Q" and m == 0:
                    wait_emptied(pe, p, "N_0")
                    wait_emptied(pe, p, "N_1")
                job = f"{name}_{m}"
                bank = work_bank(p, job)
                for half in range(2):
                    last = nc.tensor.matmul(bank[0:HALF, 0:S], w[:, half, m, :], hnT[:, half, 0:S],
                                            start=(half == 0), stop=(half == 1))
                done(job, last)

            def values(p, t):
                if p.front is None:
                    return
                job = f"V_{t}"
                bank = work_bank(p, job)
                for half in range(2):
                    if t < 2:
                        last = nc.tensor.matmul(bank[:, 0:E], hnT[:, half, P * t:P * t + P],
                                                wv_sb[:, half, :], start=(half == 0), stop=(half == 1))
                        continue
                    for j in range(4):
                        last = nc.tensor.matmul(bank[32 * j:32 * j + 32, 0:E], hnT[:, half, 2 * P:SP],
                                                wv_sb[:, half, :], start=(half == 0), stop=(half == 1))
                done(job, last)

            def one_pass(p):
                h4(p, 0)
                h4(p, 1)
                t4(p, 0)
                score_tiles(p, 0, 0, 2)
                h4(p, 2)
                t4(p, 1)
                score_tiles(p, 0, 2, 4)
                h5(p, 0)
                t4(p, 2)
                score_tiles(p, 0, 4, 7)
                h5(p, 1)
                t5(p, 0)
                score_tiles(p, 0, 7, 10)
                h5(p, 2)
                t5(p, 1)
                score_tiles(p, 0, 10, 13)
                h6(p, 0)
                t5(p, 2)
                score_tiles(p, 0, 13, 16)
                h6(p, 1)
                t6(p, 0)
                score_tiles(p, 0, 16, 19)
                h6(p, 2)
                t6(p, 1)
                score_tiles(p, 0, 19, 22)
                context(p, 0)
                t6(p, 2)
                score_tiles(p, 0, 22, 25)
                context(p, 1)
                score_tiles(p, 0, 25, TILES)
                context(p, 2)
                turn_logs(p, "L", 0)
                out_proj(p)
                score_tiles(p, 1, 0, 8)
                turn_h2(p)
                score_tiles(p, 1, 8, 10)
                for c in range(HC):
                    ffn_up(p, c)
                    if c < RING:
                        score_tiles(p, 1, 10 + c, 11 + c)
                score_tiles(p, 1, 14, 20)
                ffn_down(p, 0)
                score_tiles(p, 1, 20, 25)
                ffn_down(p, 1)
                score_tiles(p, 1, 25, TILES)
                ffn_down(p, 2)
                embed(p, 0)
                embed(p, 1)
                turn_logs(p, "M", 1)
                turn_hn(p)
                score_tiles(p, 2, 0, 4)
                project(p, "Q", 0, wq_sb)
                score_tiles(p, 2, 4, 7)
                project(p, "Q", 1, wq_sb)
                score_tiles(p, 2, 7, 10)
                project(p, "K", 0, wk_sb)
                score_tiles(p, 2, 10, 13)
                project(p, "K", 1, wk_sb)
                score_tiles(p, 2, 13, 16)
                values(p, 0)
                score_tiles(p, 2, 16, 19)
                values(p, 1)
                score_tiles(p, 2, 19, 22)
                values(p, 2)
                score_tiles(p, 2, 22, TILES)

            pe.wait_ge(prep_step, PREP_STEPS)
            run_passes(pe, B, one_pass)

        @block.scalar
        def _(act):
            def exp_tiles(p, which, lo, hi):
                if p.mid is None:
                    return
                for k in range(lo, hi):
                    slot = TILES * which + k
                    col = column_of(k)
                    if which < 2:
                        act.wait_ge(max_ready, 2 * TILES * p.mid + slot + 1)
                    else:
                        wait_scores(act, p.mid, slot)
                    neg, total, dst = ((neg_r, rho, junk[:, slot % RING, :]), (neg_c, kappa, G[:, k, :]),
                                       (None, sigma, PL[:, k, :]))[which]
                    bias = {} if neg is None else {"bias": neg[:, col:col + 1]}
                    nc.scalar.activation(dst, score[slot % RING][:, 0:S], ACT.Exp,
                                         accum_out=total[:, col:col + 1],
                                         **bias).then_inc(score_free[slot % RING], 1)

            def log_sums(p, n):
                if p.mid is not None:
                    wait_exp(act, p.mid, TILES * (n + 1) - 1)
                    nc.scalar.activation(ln_sum[:], (rho, kappa)[n][:], ACT.Ln).then_inc(ln_ready, 1)

            def a_rows(p, g):
                if p.back is None:
                    return
                job = f"H5_{g}"
                bank = wait_full(act, p, job)
                nc.scalar.activation(ln_row[:, g, :], bank[:, 0:S], ACT.Ln)\
                    .then_inc(work_free[BANK[job]], 1)
                wait_emptied(act, p, job)
                nc.scalar.activation(a_row[:, g, 0:S], ln_row[:, g, :], ACT.Exp, scale=-1.0)\
                    .then_inc(a_row_ready, 1)

            def copy_out(p, job, dst):
                if p.active(job):
                    bank = wait_full(act, p, job)
                    nc.scalar.activation(dst, bank[0:dst.shape[0], 0:S], ACT.Copy)\
                        .then_inc(work_free[BANK[job]], 1)

            def gelu(p, c):
                if p.back is None:
                    return
                job = f"G_{c}"
                bank = wait_full(act, p, job)
                nc.scalar.activation(gT[:, c, :], bank[:, 0:S], ACT.Gelu_apprx_tanh,
                                     bias=b0_sb[:, c:c + 1]).then_inc(work_free[BANK[job]], 1)

            def one_pass(p):
                copy_out(p, "H4_0", sums[:, 0, 0:S])
                copy_out(p, "H4_1", sums[:, 1, 0:S])
                exp_tiles(p, 0, 0, 2)
                copy_out(p, "H4_2", sums[:, 2, 0:S])
                exp_tiles(p, 0, 2, 4)
                a_rows(p, 0)
                exp_tiles(p, 0, 4, 7)
                a_rows(p, 1)
                exp_tiles(p, 0, 7, 10)
                a_rows(p, 2)
                exp_tiles(p, 0, 10, 13)
                copy_out(p, "H6_0", sums[:, 0, 0:S])
                exp_tiles(p, 0, 13, 16)
                copy_out(p, "H6_1", sums[:, 1, 0:S])
                exp_tiles(p, 0, 16, 19)
                copy_out(p, "H6_2", sums[:, 2, 0:S])
                exp_tiles(p, 0, 19, TILES)
                log_sums(p, 0)
                exp_tiles(p, 1, 0, 8)
                copy_out(p, "X_0", h2T[:, 0, :])
                copy_out(p, "X_1", h2T[:, 1, :])
                exp_tiles(p, 1, 8, 10)
                for c in range(HC):
                    gelu(p, c)
                if p.back is not None:
                    act.preload_act_table_set("natural_log_exp_and_others")
                exp_tiles(p, 1, 10, TILES)
                log_sums(p, 1)
                copy_out(p, "N_0", hnT[:, 0, 0:S])
                copy_out(p, "N_1", hnT[:, 1, 0:S])
                exp_tiles(p, 2, 0, TILES)

            act.preload_act_table_set("natural_log_exp_and_others")
            act.wait_ge(prep_step, PREP_STEPS)
            run_passes(act, B, one_pass)

        @block.vector
        def _(dve):
            count = [0]

            def prep(ins):
                count[0] += 1
                ins.then_inc(prep_step, 1)
                dve.wait_ge(prep_step, count[0])

            dve.wait_ge(weights_in, 16 * WEIGHT_DMAS)
            dve.wait_ge(pool_prep, POOL_PREPS)
            prep(nc.vector.tensor_copy(ident_bf[:], ident[:]))
            prep(nc.vector.memset(q_stack[L_ROW:STACK, :, :], 1.0))
            prep(nc.vector.memset(k_stack[L_ROW:STACK, :, :], 1.0))
            prep(nc.vector.reduce_sum(mask_rest[:], mask12[:, 8:12], AX_X))
            prep(nc.vector.tensor_scalar(pad_one[:], mask_rest[:], -1.0, 1.0, ALU.mult, ALU.add))
            prep(nc.vector.tensor_scalar(pad_neg[:], pad_one[:], NEG, None, ALU.mult))
            for i in range(3):
                prep(nc.vector.tensor_scalar(pair[:, 3 * i:3 * i + 3], alpha_sb[:, 3:6],
                                             alpha_sb[:, i:i + 1], None, ALU.mult))
            prep(nc.vector.memset(coef[:], 0.0))
            for i in (2, 1, 0):
                for j in range(3):
                    acc = coef[:, i + 1, :] if j == 0 and i < 2 else coef[:, i, :]
                    n = 3 * i + j
                    prep(nc.vector.scalar_tensor_tensor(out=coef[:, i, :], in0=below[:, n, :],
                                                        scalar=pair[:, n:n + 1], in1=acc,
                                                        op0=ALU.mult, op1=ALU.add))
            prep(nc.vector.tensor_tensor(b0_sb[:], b0_sb[:], coef[:, 0, :], ALU.mult))
            lo = 0
            for i, e in enumerate(EMBED_CHOICES):
                prep(nc.vector.tensor_tensor(w1_sb[:, :, lo:e], w1_sb[:, :, lo:e],
                                             coef[:, i, :].unsqueeze(2).to_broadcast([P, HC, e - lo]),
                                             ALU.mult))
                prep(nc.vector.reduce_sum(coef_out[:, i:i + 1], pair[:, 3 * i:9], AX_X))
                prep(nc.vector.tensor_scalar(b1_sb[:, lo:e], b1_sb[:, lo:e], coef_out[:, i:i + 1], None,
                                             ALU.mult))
                lo = e
            prep(nc.vector.memset(coef_row[:], 0.0))
            for i, e in enumerate(EMBED_CHOICES):
                for j, r in enumerate(RATIO_CHOICES):
                    for half in range(2):
                        rows = min(max(e - HALF * half, 0), HALF)
                        if rows:
                            c = coef_row[0:rows, half, 0:r * e]
                            n = 3 * i + j
                            prep(nc.vector.tensor_scalar(c, c, pair[0:rows, n:n + 1], None, ALU.add))
            prep(nc.vector.tensor_tensor(w0_sb[:], w0_sb[:], coef_row[:], ALU.mult))
            assert count[0] == PREP_STEPS, count[0]

            nc.vector.memset(fence[:], 0.0).then_inc(out_stored, OUT_FREE)
            steps = {}

            def step(p, stage, ins):
                steps[stage] += 1
                ins.then_inc(vector_step[stage], 1)
                dve.wait_ge(vector_step[stage], p.images[stage] * LINKS[stage] + steps[stage])

            def max_tiles(p, which, lo, hi):
                if p.mid is None:
                    return
                for k in range(lo, hi):
                    slot = TILES * which + k
                    col = column_of(k)
                    wait_scores(dve, p.mid, slot)
                    nc.vector.tensor_reduce((neg_r, neg_c)[which][:, col:col + 1],
                                            score[slot % RING][:, 0:S], op=ALU.max, axis=AX_X,
                                            negate=True).then_inc(max_ready, 1)

            def logs(p, n):
                if p.mid is None:
                    return
                dve.wait_ge(ln_ready, 2 * p.mid + n + 1)
                step(p, "mid", nc.vector.tensor_tensor(log_f[:], (neg_r, neg_c)[n][:], ln_sum[:],
                                                       ALU.subtract))
                if n == 0:
                    f = log_f[:, 2 * H:TILES]
                    step(p, "mid", nc.vector.tensor_scalar(f, f, mask_rest[:], pad_neg[:],
                                                           ALU.mult, ALU.add))
                def whole(t):
                    return t[:, 0:2 * H].rearrange("p (c h) -> p c h", c=2)

                def rest(t):
                    return t[:, 2 * H:TILES]

                split_at = 2 * PARTS * H
                parts = [(log_parts[:, 0:split_at].rearrange("p (c n h) -> p c n h", c=2, n=PARTS)[:, :, i, :],
                          log_parts[:, split_at + GROUPS * i:split_at + GROUPS * i + GROUPS])
                         for i in range(PARTS)]
                both = (whole, rest)
                for i, view in enumerate(both):
                    last = nc.vector.tensor_copy(parts[0][i], view(log_f))
                step(p, "mid", last)
                for i, view in enumerate(both):
                    last = nc.vector.tensor_tensor(view(log_r), view(log_f), parts[0][i], ALU.subtract)
                step(p, "mid", last)
                for i, view in enumerate(both):
                    last = nc.vector.tensor_copy(parts[1][i], view(log_r))
                step(p, "mid", last)
                for i, view in enumerate(both):
                    last = nc.vector.tensor_tensor(parts[2][i], view(log_r), parts[1][i], ALU.subtract)
                last.then_inc(log_ready, 1)

            def log_rows_out(p, job, n):
                if p.mid is None:
                    return
                wait(dve, log_stacked, 32 * (2 * p.mid + n))
                bank = wait_full(dve, p, job)[:, :].bitcast(BF16)
                nc.vector.tensor_copy(log_rows[:], bank[0:PARTS * H, 0:2 * P])
                nc.vector.tensor_copy(log_rest[:], bank[0:PARTS * GROUPS, 2 * P:3 * P])\
                    .then_inc(work_free[BANK[job]], 1)

            def by_head(t, g):
                return t[:, 0:2 * H].rearrange("p (c h) -> p c h", c=2)[:, :, 4 * g:4 * g + 4]

            def kappa_weights(p):
                if p.mid is None:
                    return
                step(p, "mid", nc.vector.reciprocal(rest_tmp[:], kappa[:, 2 * H:TILES]))
                for g in range(GROUPS):
                    nc.vector.reciprocal(inv_kappa[:, g, 0:8].rearrange("p (c j) -> p c j", c=2),
                                         by_head(kappa, g))
                nc.vector.tensor_tensor(inv_kappa[:, :, 8:12],
                                        rest_tmp[:].unsqueeze(2).to_broadcast([P, GROUPS, 4]),
                                        mask12[:, 8:12].unsqueeze(1).to_broadcast([P, GROUPS, 4]),
                                        ALU.mult).then_inc(kappa_ready, 1)

            def first_half_weights(p, g):
                if p.back is None:
                    return
                wait_exp(dve, p.back, 2 * TILES + 9 * g + 8)
                nc.vector.reciprocal(w_a[:, g, 0:8].rearrange("p (c j) -> p c j", c=2),
                                     by_head(sigma, g))
                rest = sigma_rest[:, g:g + 1]
                step(p, "back", nc.vector.tensor_scalar(rest, sigma[:, 2 * H + g:2 * H + g + 1],
                                                        pad_one[:], None, ALU.add))
                step(p, "back", nc.vector.reciprocal(rest, rest))
                nc.vector.tensor_scalar(w_a[:, g, 8:12], mask12[:, 8:12], rest, None, ALU.mult)\
                    .then_inc(first_weights, 1)

            def turned(p, job):
                bank = wait_full(dve, p, job)
                return bank[:, 0:3 * P].rearrange("p (c j r) -> p c j r", c=3, r=32)[:, :, :, 0]

            def three(t, g):
                return t[:, g, :].rearrange("p (c j) -> p c j", c=3)

            def t4(p, g):
                if p.back is None:
                    return
                job = f"T4_{g}"
                nc.vector.reciprocal(three(recip12, g), turned(p, job)).then_inc(work_free[BANK[job]], 1)
                wait_emptied(dve, p, job)
                if g == 0:
                    dve.wait_ge(kappa_ready, p.back + 1)
                nc.vector.tensor_tensor(w_b[:, g, :], recip12[:, g, :], inv_kappa[:, g, :],
                                        ALU.mult).then_inc(half_weights, 1)

            def t5(p, g):
                if p.back is not None:
                    job = f"T5_{g}"
                    nc.vector.tensor_tensor(three(w_a2, g), turned(p, job),
                                            mask12[:].rearrange("p (c j) -> p c j", c=3),
                                            ALU.mult).then_inc(work_free[BANK[job]], 1)

            def t6(p, g):
                if p.back is None:
                    return
                job = f"T6_{g}"
                nc.vector.reciprocal(three(recip12, g), turned(p, job)).then_inc(work_free[BANK[job]], 1)
                wait_emptied(dve, p, job)
                step(p, "back", nc.vector.tensor_tensor(w_b2[:, g, :], recip12[:, g, :],
                                                        inv_kappa[:, g, :], ALU.mult))
                if g == 0:
                    dve.wait_ge(cur_ready, 5 * p.back + 5)
                heads = v_cur[:, :, 4 * D * g:4 * D * g + 4 * D]
                nc.vector.tensor_tensor(
                    v_w[:, g, :, 0:D].rearrange("p (c j) d -> p c j d", c=3),
                    heads.rearrange("p c (j d) -> p c j d", j=4),
                    three(w_b2, g).unsqueeze(3).to_broadcast([P, 3, 4, D]),
                    ALU.mult).then_inc(v_weighted, 1)

            def context(p, g):
                if p.back is None:
                    return
                job = f"C_{g}"
                dve.wait_ge(a_row_ready, 3 * p.back + g + 1)
                bank = wait_full(dve, p, job)
                nc.vector.tensor_tensor(ctxT[:, g, :], bank[:, 0:S], a_row[:, g, 0:S], ALU.mult)\
                    .then_inc(work_free[BANK[job]], 1)

            def statistics(p, stage, src, stats, mv, eps, ready):
                for t in range(3):
                    last = nc.vector.bn_stats(stats[0:ROWS[t], t, :], src[0:ROWS[t], t, :])
                step(p, stage, last)
                nc.vector.memset(fence[:], 0.0)
                for t in range(3):
                    last = nc.vector.bn_aggr(mv[0:ROWS[t], t, :], stats[0:ROWS[t], t, :])
                step(p, stage, last)
                nc.vector.tensor_scalar(mv[:, :, 1], mv[:, :, 1], eps, None, ALU.add)\
                    .then_inc(ready, 1)

            def output_tokens(p):
                if p.back is None:
                    return
                for t in range(3):
                    job = f"W_{t}"
                    bank = wait_full(dve, p, job)
                    rows = ROWS[t]
                    nc.vector.tensor_tensor(y_sb[0:rows, t, :], bank[0:rows, 0:E],
                                            hbo_cur[0:rows, t, :], ALU.add)\
                        .then_inc(work_free[BANK[job]], 1)
                wait_emptied(dve, p, "W_2")
                statistics(p, "back", y_sb, stats_b, mv_b, ATTN_EPS, var_ready["b"])

            def residual(p):
                if p.back is None:
                    return
                dve.wait_ge(rstd_ready["b"], p.back + 1)
                if p.mid is not None or True:
                    pass
                for t in range(3):
                    rows = ROWS[t]
                    last = nc.vector.scalar_tensor_tensor(
                        out=y_sb[0:rows, t, :], in0=y_sb[0:rows, t, :], scalar=mv_b[0:rows, t, 0:1],
                        in1=ln_g_sb[0:rows, :], op0=ALU.subtract, op1=ALU.mult)
                step(p, "back", last)
                for t in range(3):
                    rows = ROWS[t]
                    last = nc.vector.scalar_tensor_tensor(
                        out=h2_sb[0:rows, t, :], in0=y_sb[0:rows, t, :], scalar=rstd_b[0:rows, t:t + 1],
                        in1=hlb_cur[0:rows, t, :], op0=ALU.mult, op1=ALU.add)
                last.then_inc(h2_ready, 1)
                dve.wait_ge(h2_ready, p.back + 1)
                statistics(p, "back", h2_sb, stats_c, mv_c, LN_EPS, var_ready["c"])

            def normalise(p, image, src, dst, mv, rstd, which, ready):
                dve.wait_ge(rstd_ready[which], image + 1)
                for t in range(3):
                    rows = ROWS[t]
                    last = nc.vector.tensor_scalar(dst[0:rows, t, :], src[0:rows, t, :],
                                                   mv[0:rows, t, 0:1], rstd[0:rows, t:t + 1],
                                                   ALU.subtract, ALU.mult)
                last.then_inc(ready, 1)

            def ffn_out(p, t):
                if p.back is None:
                    return
                job = f"O_{t}"
                if t == 0:
                    dve.wait_ge(h2b_ready, 2 * p.back + 2)
                    dve.wait_ge(out_stored, 32 * p.back + OUT_FREE)
                bank = wait_full(dve, p, job)
                rows = ROWS[t]
                nc.vector.tensor_tensor(out_sb[0:rows, t, :], bank[0:rows, 0:E], h2b_sb[0:rows, t, :],
                                        ALU.add).then_inc(work_free[BANK[job]], 1)

            def embed(p):
                if p.front is None:
                    return
                if p.mid is not None:
                    dve.wait_ge(cur_ready, 5 * p.mid + 5)
                for t, rows in enumerate((P, NPATCH - P)):
                    job = f"E_{t}"
                    bank = wait_full(dve, p, job)
                    nc.vector.tensor_tensor(h_sb[0:rows, t, :], bank[0:rows, 0:E], tok_b_sb[0:rows, :],
                                            ALU.add).then_inc(work_free[BANK[job]], 1)
                wait_emptied(dve, p, "E_0")
                wait_emptied(dve, p, "E_1")
                dve.wait_ge(txt_in, 32 * (p.front + 1))
                statistics(p, "front", h_sb, stats_f, mv_f, LN_EPS, var_ready["f"])

            def split(p, name, m, bias, scale):
                if p.front is None:
                    return
                job = f"{name}_{m}"
                i = 2 * (name == "K") + m
                bank = wait_full(dve, p, job)
                nc.vector.tensor_scalar(qk_f[:, i, 0:S], bank[0:HALF, 0:S], bias[:, m:m + 1], scale,
                                        ALU.add, ALU.mult).then_inc(work_free[BANK[job]], 1)
                wait_emptied(dve, p, job)
                if i == 0:
                    wait(dve, stacked, 16 * 4 * NBLK * p.front)
                part = [qk_parts[:, i, n, 0:S] for n in range(PARTS)]
                step(p, "front", nc.vector.tensor_copy(part[0], qk_f[:, i, 0:S]))
                step(p, "front", nc.vector.tensor_tensor(qk_r[:, i, 0:S], qk_f[:, i, 0:S], part[0],
                                                         ALU.subtract))
                step(p, "front", nc.vector.tensor_copy(part[1], qk_r[:, i, 0:S]))
                nc.vector.tensor_tensor(part[2], qk_r[:, i, 0:S], part[1], ALU.subtract)\
                    .then_inc(parts_ready, 1)

            def values(p):
                if p.front is None:
                    return
                for t in range(3):
                    job = f"V_{t}"
                    bank = wait_full(dve, p, job)
                    nc.vector.tensor_tensor(v_sb[:, t, :], bank[:, 0:E], bv_sb[:], ALU.add)\
                        .then_inc(work_free[BANK[job]], 1)
                wait_emptied(dve, p, "V_2")
                nc.vector.memset(fence[:], 0.0).then_inc(v_ready, 1)

            def one_pass(p):
                steps.update(dict.fromkeys(LINKS, 0))
                for g in range(GROUPS):
                    first_half_weights(p, g)
                max_tiles(p, 0, 0, 2)
                t4(p, 0)
                max_tiles(p, 0, 2, 4)
                t4(p, 1)
                max_tiles(p, 0, 4, 5)
                t4(p, 2)
                max_tiles(p, 0, 5, 7)
                t5(p, 0)
                max_tiles(p, 0, 7, 10)
                t5(p, 1)
                max_tiles(p, 0, 10, 13)
                t5(p, 2)
                max_tiles(p, 0, 13, 16)
                t6(p, 0)
                max_tiles(p, 0, 16, 19)
                t6(p, 1)
                max_tiles(p, 0, 19, 22)
                context(p, 0)
                t6(p, 2)
                max_tiles(p, 0, 22, 25)
                context(p, 1)
                max_tiles(p, 0, 25, TILES)
                context(p, 2)
                logs(p, 0)
                log_rows_out(p, "L", 0)
                output_tokens(p)
                residual(p)
                max_tiles(p, 1, 0, 4)
                if p.back is not None:
                    normalise(p, p.back, h2_sb, h2n_sb, mv_c, rstd_c, "c", h2n_ready)
                max_tiles(p, 1, 4, 20)
                ffn_out(p, 0)
                max_tiles(p, 1, 20, 25)
                ffn_out(p, 1)
                max_tiles(p, 1, 25, TILES)
                ffn_out(p, 2)
                logs(p, 1)
                embed(p)
                log_rows_out(p, "M", 1)
                kappa_weights(p)
                if p.front is not None:
                    normalise(p, p.front, h_sb, hn_sb, mv_f, rstd_f, "f", hn_ready)
                split(p, "Q", 0, bq_sb, D ** -0.5)
                split(p, "Q", 1, bq_sb, D ** -0.5)
                split(p, "K", 0, bk_sb, 1.0)
                split(p, "K", 1, bk_sb, 1.0)
                values(p)
                for stage, n in steps.items():
                    assert p.images[stage] is None or n == LINKS[stage], (stage, n)

            run_passes(dve, B, one_pass)


def lay_out(inputs):
    import numpy as np

    a = {k: np.asarray(v) for k, v in inputs.items()}
    B = a["x"].shape[0]
    x = a["x"].reshape(B, 3, 14, 16, 14, 16).transpose(0, 1, 3, 5, 2, 4).reshape(B, KC, P, NPATCH)

    def halves(w):
        return w.reshape(2, HALF, -1).transpose(1, 0, 2)

    def qk(w):
        w = w.reshape(2, HALF, 2, HH, D).transpose(1, 0, 2, 4, 3)
        return w.reshape(HALF, 2, 2, HALF)

    def qk_bias(b):
        return b.reshape(2, HH, D).transpose(2, 1, 0).reshape(HALF, 2)

    d = {
        "x": x.transpose(0, 2, 1, 3),
        "txt": a["txt"],
        "tok_w": a["L0_tok_W"].reshape(KC, P, E).transpose(1, 0, 2),
        "tok_b": a["L0_tok_b"],
        "cls": a["L0_tok_cls_token"].reshape(1, E),
        "wq": qk(a["L0_attn_Wq"]), "wk": qk(a["L0_attn_Wk"]), "wv": halves(a["L0_attn_Wv"]),
        "wo": a["L0_attn_Wo"].reshape(GROUPS, 4, D, E).transpose(1, 2, 0, 3),
        "bq": qk_bias(a["L0_attn_bq"]), "bk": qk_bias(a["L0_attn_bk"]),
        "bv": a["L0_attn_bv"], "bo": a["L0_attn_bo"],
        "ln_g": a["L0_attn_ln_g"], "ln_b": a["L0_attn_ln_b"],
        "w_fc": halves(a["L0_ffn_w_fc"].T),
        "b_fc": a["L0_ffn_b_fc"].reshape(HC, P).T,
        "w_proj": a["L0_ffn_w_proj"].T.reshape(HC, P, E).transpose(1, 0, 2),
        "b_proj": a["L0_ffn_b_proj"],
        "alpha_e": a["L0_ffn_alpha_e"], "alpha_r": a["L0_ffn_alpha_r"],
    }
    return {k: np.ascontiguousarray(v) for k, v in d.items()}


def kernel(**inputs):
    import numpy as np
    import concourse.bacc as bacc
    from concourse.bass_utils import run_bass_kernel_spmd

    nc = bacc.Bacc("TRN2", target_bir_lowering=False, num_devices=1)
    arrays = {f"in_{k}": v for k, v in lay_out(inputs).items()}
    args = {k[3:]: nc.dram_tensor(k, v.shape, mybir.dt.from_np(v.dtype), kind="ExternalInput").ap()
            for k, v in arrays.items()}
    B = arrays["in_x"].shape[0]
    out = nc.dram_tensor("out_tokens", (B, S, E), F32, kind="ExternalOutput").ap()
    early_fusion_kernel(nc, out=out, **args)
    got = np.asarray(run_bass_kernel_spmd(nc, [arrays], core_ids=[0]).results[0]["out_tokens"])
    return np.concatenate([got[:, NPATCH:NPATCH + 1], got[:, :NPATCH], got[:, NPATCH + 1:]], axis=1)
```

```python
from contextlib import ExitStack

import concourse.bass as bass
from concourse import mybir

ALU = mybir.AluOpType
ACT = mybir.ActivationFunctionType
AX_X = mybir.AxisListType.X
F32 = mybir.dt.float32
BF16 = mybir.dt.bfloat16

P = 128
E = 192
H = 12
D = E // H
S = 274
NPATCH = 196
NTXT = 77
KC = 768 // P
REST = S - 2 * P
SP = 2 * P + 32
CLS_ROW = NPATCH - P
HALF = E // 2
HH = H // 2
GROUPS = H // 4
TILES = 9 * GROUPS
HID = 768
HC = HID // P
PARTS = 3
Q_BLOCKS = (0, 0, 1, 1, 0, 2)
K_BLOCKS = (0, 1, 0, 1, 2, 0)
NBLK = len(Q_BLOCKS)
L_ROW = NBLK * D
M_ROW = L_ROW + PARTS
STACK = M_ROW + PARTS
PREP_STEPS = 46
NEG = -1.0e30
LN_EPS, ATTN_EPS = 1e-5, 1e-12
EMBED_CHOICES = (96, 144, 192)
RATIO_CHOICES = (2, 3, 4)

JOBS = (
    "T4_0", "T4_1", "H5_0", "T4_2", "H5_1", "T5_0", "H5_2", "T5_1", "H6_0", "T5_2", "H6_1",
    "T6_0", "H6_2", "T6_1", "C_0", "T6_2", "C_1", "L", "C_2", "W_0", "W_1", "W_2", "E_0", "E_1",
    "X_0", "X_1", "G_0", "G_1", "G_2", "G_3", "G_4", "G_5", "N_0", "N_1", "O_0", "M", "O_1",
    "O_2", "Q_0", "Q_1", "K_0", "K_1", "V_0", "V_1", "H4_0", "V_2", "H4_1", "H4_2"
)
NBANK = 4
STAGE = {n: "mid" if n[0] in "LM" or n[:2] == "H4" else "front" if n[0] in "ENQKV" else "back" for n in JOBS}
BANK = {n: i % NBANK for i, n in enumerate(JOBS)}
RING = 4
RING_USES = [len(range(r, 3 * TILES, RING)) for r in range(RING)]

LINKS = {"front": 2 + 4 * 3, "mid": 10 + 2 * GROUPS, "back": 14 - 2 * GROUPS}


def tile_of(k):
    g, i = divmod(k, 9)
    return (g, None, 2) if i == 8 else (g, 4 * g + i // 2, i % 2)


def column_of(k):
    g, h, c = tile_of(k)
    return 2 * H + g if h is None else c * H + h


class Pass:

    def __init__(self, images, banks_before, last_active=None):
        self.images = images
        self.banks_before = banks_before
        self.last_active = last_active
        self.back, self.mid, self.front = images["back"], images["mid"], images["front"]

    def active(self, job):
        return self.images[STAGE[job]] is not None

    def uses_before(self, job):
        mine = [n for n in JOBS if self.active(n) and BANK[n] == BANK[job]]
        return self.banks_before[BANK[job]] + mine.index(job)

    def uses_last_pass(self, job):
        later = [n for n in JOBS[JOBS.index(job) + 1:]
                 if BANK[n] == BANK[job] and self.last_active[STAGE[n]]]
        return self.banks_before[BANK[job]] - len(later)

    def uses(self):
        return [sum(self.active(n) and BANK[n] == r for n in JOBS) for r in range(NBANK)]


def images_of(it, B):
    return {"back": it if 0 <= it < B else None, "mid": it + 1 if 0 <= it + 1 < B else None,
            "front": it + 2 if 0 <= it + 2 < B else None}


def run_passes(engine, B, one_pass):
    before = [0] * NBANK

    def last_active(it):
        return {stage: image is not None for stage, image in images_of(it - 1, B).items()}

    def fixed(it):
        nonlocal before
        p = Pass(images_of(it, B), list(before), last_active(it))
        one_pass(p)
        before = [a + b for a, b in zip(before, p.uses())]

    for it in range(-2, 1):
        fixed(it)
    full = Pass({"back": 0, "mid": 1, "front": 2}, before).uses()
    with engine.Fori(1, B - 2) as it:
        one_pass(Pass({"back": it, "mid": it + 1, "front": it + 2},
                      [it * n + a - n for n, a in zip(full, before)], last_active(1)))
    before = [a + (B - 3) * n for a, n in zip(before, full)]
    fixed(B - 2)
    fixed(B - 1)


def early_fusion_kernel(nc, x, txt, tok_w, tok_b, cls, wq, wk, wv, wo, bq, bk, bv, bo, ln_g, ln_b,
                        w_fc, b_fc, w_proj, b_proj, alpha_e, alpha_r, out):
    B = x.shape[0]
    with ExitStack() as ctx:
        def sb(name, shape, dt=F32):
            return ctx.enter_context(nc.sbuf_tensor(name, shape, dt))

        def sem(name):
            return ctx.enter_context(nc.semaphore(name))

        ident = sb("ident", [P, P])
        ident_bf = sb("ident_bf", [P, P], BF16)
        mask12 = sb("mask12", [P, 12])
        mask_rest = sb("mask_rest", [P, 1])
        pad_one = sb("pad_one", [P, 1])
        pad_neg = sb("pad_neg", [P, 1])
        minus_half = sb("minus_half", [P, 3])
        tok_w_sb = sb("tok_w_sb", [P, KC, E])
        wq_sb = sb("wq_sb", [HALF, 2, 2, HALF])
        wk_sb = sb("wk_sb", [HALF, 2, 2, HALF])
        wv_sb = sb("wv_sb", [HALF, 2, E])
        wo_sb = sb("wo_sb", [P, GROUPS, E])
        w0_sb = sb("w0_sb", [HALF, 2, HID])
        w1_sb = sb("w1_sb", [P, HC, E])
        bq_sb = sb("bq_sb", [HALF, 2])
        bk_sb = sb("bk_sb", [HALF, 2])
        tok_b_sb = sb("tok_b_sb", [P, E])
        bv_sb = sb("bv_sb", [P, E])
        bo_sb = sb("bo_sb", [P, E])
        ln_g_sb = sb("ln_g_sb", [P, E])
        ln_b_sb = sb("ln_b_sb", [P, E])
        b1_sb = sb("b1_sb", [P, E])
        b0_sb = sb("b0_sb", [P, HC])
        alpha_sb = sb("alpha_sb", [P, 6])
        pair = sb("pair", [P, 9])
        below = sb("below", [P, 9, HC])
        coef = sb("coef", [P, 3, HC])
        coef_row = sb("coef_row", [HALF, 2, HID])
        coef_out = sb("coef_out", [P, 3])
        fence = sb("fence", [P, 1])
        pool_fence = sb("pool_fence", [P, 1])

        x_sb = sb("x_sb", [P, KC, NPATCH])
        h_sb = sb("h_sb", [P, 3, E])
        hn_sb = sb("hn_sb", [P, 3, E])
        hnT = sb("hnT", [HALF, 2, SP])
        qk_f = sb("qk_f", [HALF, 4, SP])
        qk_r = sb("qk_r", [HALF, 4, SP])
        qk_parts = sb("qk_parts", [HALF, 2, PARTS, 2, SP], BF16)
        v_sb = sb("v_sb", [P, 3, E])
        stats_f = sb("stats_f", [P, 3, 6])
        mv_f = sb("mv_f", [P, 3, 2])
        rstd_f = sb("rstd_f", [P, 3])
        q_stack = sb("q_stack", [STACK, H, SP], BF16)
        k_stack = sb("k_stack", [STACK, H, SP], BF16)
        neg_r = sb("neg_r", [P, TILES])
        neg_c = sb("neg_c", [P, TILES])
        rho = sb("rho", [P, TILES])
        kappa = sb("kappa", [P, TILES])
        sigma = sb("sigma", [P, TILES])
        ln_sum = sb("ln_sum", [P, TILES])
        log_f = sb("log_f", [P, TILES])
        log_r = sb("log_r", [P, TILES])
        log_parts = sb("log_parts", [P, PARTS * TILES], BF16)
        log_rows = sb("log_rows", [PARTS * H, 2 * P], BF16)
        log_rest = sb("log_rest", [PARTS * GROUPS, P], BF16)
        junk = sb("junk", [P, RING, S], BF16)
        G = sb("G", [P, TILES, S])
        PL = sb("PL", [P, TILES, S])
        rest_tmp = sb("rest_tmp", [P, GROUPS])
        sigma_rest = sb("sigma_rest", [P, GROUPS])
        inv_kappa = sb("inv_kappa", [P, GROUPS, 12])
        w_a = sb("w_a", [P, GROUPS, 12])
        w_b = sb("w_b", [P, GROUPS, 12])
        w_a2 = sb("w_a2", [P, GROUPS, 12])
        w_b2 = sb("w_b2", [P, GROUPS, 12])
        recip12 = sb("recip12", [P, GROUPS, 12])
        sums = sb("sums", [P, GROUPS, SP])
        ln_row = sb("ln_row", [P, GROUPS, S])
        a_row = sb("a_row", [P, GROUPS, SP])
        v_cur = sb("v_cur", [P, 3, E])
        v_w = sb("v_w", [P, GROUPS, 12, 32])
        ctxT = sb("ctxT", [P, GROUPS, S])
        hbo_next = sb("hbo_next", [P, 3, E])
        hlb_next = sb("hlb_next", [P, 3, E])
        hbo_cur = sb("hbo_cur", [P, 3, E])
        hlb_cur = sb("hlb_cur", [P, 3, E])
        y_sb = sb("y_sb", [P, 3, E])
        h2_sb = sb("h2_sb", [P, 3, E])
        h2n_sb = sb("h2n_sb", [P, 3, E])
        h2b_sb = sb("h2b_sb", [P, 3, E])
        stats_b = sb("stats_b", [P, 3, 6])
        mv_b = sb("mv_b", [P, 3, 2])
        rstd_b = sb("rstd_b", [P, 3])
        stats_c = sb("stats_c", [P, 3, 6])
        mv_c = sb("mv_c", [P, 3, 2])
        rstd_c = sb("rstd_c", [P, 3])
        h2T = sb("h2T", [HALF, 2, S])
        gT = sb("gT", [P, HC, S])
        out_sb = sb("out_sb", [P, 3, E])

        score = [ctx.enter_context(nc.psum_tensor(f"score{r}", [P, 512], F32)) for r in range(RING)]
        work = [ctx.enter_context(nc.psum_tensor(f"work{r}", [P, 512], F32)) for r in range(NBANK)]

        weights_in = sem("weights_in")
        pool_prep = sem("pool_prep")
        prep_step = sem("prep_step")
        x_in = sem("x_in")
        txt_in = sem("txt_in")
        score_full = [sem(f"score_full{r}") for r in range(RING)]
        score_free = [sem(f"score_free{r}") for r in range(RING)]
        work_full = [sem(f"work_full{r}") for r in range(NBANK)]
        work_free = [sem(f"work_free{r}") for r in range(NBANK)]
        max_ready = sem("max_ready")
        ln_ready = sem("ln_ready")
        log_ready = sem("log_ready")
        log_stacked = sem("log_stacked")
        parts_ready = sem("parts_ready")
        stacked = sem("stacked")
        var_ready = {s: sem(f"var_ready_{s}") for s in "fbc"}
        rstd_ready = {s: sem(f"rstd_ready_{s}") for s in "fbc"}
        hn_ready = sem("hn_ready")
        kappa_ready = sem("kappa_ready")
        v_ready = sem("v_ready")
        next_ready = sem("next_ready")
        cur_ready = sem("cur_ready")
        first_weights = sem("first_weights")
        half_weights = sem("half_weights")
        a_row_ready = sem("a_row_ready")
        v_weighted = sem("v_weighted")
        h2_ready = sem("h2_ready")
        h2n_ready = sem("h2n_ready")
        h2b_ready = sem("h2b_ready")
        out_stored = sem("out_stored")
        vector_step = {s: sem(f"vector_step_{s}") for s in LINKS}

        ROWS = (P, P, REST)
        WIDE = ((slice(0, 2), P), (slice(2, 3), REST))

        def spread(t, rows, n):
            return t[0:rows, :].unsqueeze(1).to_broadcast([rows, n, E])

        def wait(engine, semaphore, value):
            if not (isinstance(value, int) and value == 0):
                engine.wait_ge(semaphore, value)

        def wait_full(engine, p, job):
            engine.wait_ge(work_full[BANK[job]], p.uses_before(job) + 1)
            return work[BANK[job]]

        def wait_emptied(engine, p, *jobs):
            for job in {BANK[n]: n for n in sorted(jobs, key=JOBS.index)}.values():
                engine.wait_ge(work_free[BANK[job]], p.uses_before(job) + 1)

        def wait_exp(engine, image, slot):
            engine.wait_ge(score_free[slot % RING], image * RING_USES[slot % RING] + slot // RING + 1)

        def wait_scores(engine, image, slot):
            engine.wait_ge(score_full[slot % RING], image * RING_USES[slot % RING] + slot // RING + 1)

        OUT_FREE = 1
        WEIGHT_DMAS = 9 + 6 + 3 + 4
        POOL_PREPS = 27

        block = ctx.enter_context(nc.Block())

        @block.sync
        def _(sp):
            for dst, src in ((tok_w_sb, tok_w), (wq_sb, wq), (wk_sb, wk), (wv_sb, wv), (w0_sb, w_fc),
                             (w1_sb, w_proj), (bq_sb, bq), (bk_sb, bk), (b0_sb, b_fc)):
                sp.dma_start(dst[:], src).then_inc(weights_in, 16)
            for dst, src in ((tok_b_sb, tok_b), (bv_sb, bv), (bo_sb, bo), (ln_g_sb, ln_g),
                             (ln_b_sb, ln_b), (b1_sb, b_proj)):
                sp.dma_start(dst[:], src.partition_broadcast(P)).then_inc(weights_in, 16)
            sp.dma_start(alpha_sb[:, 0:3], alpha_e.partition_broadcast(P)).then_inc(weights_in, 16)
            sp.dma_start(alpha_sb[:, 3:6], alpha_r.partition_broadcast(P)).then_inc(weights_in, 16)
            sp.dma_start(h_sb[CLS_ROW:CLS_ROW + 1, 1, :], cls).then_inc(weights_in, 16)
            sp.wait_ge(pool_prep, 1)
            for j in range(4):
                sp.dma_start(wo_sb[32 * j:32 * j + D, :, :], wo[j]).then_inc(weights_in, 16)
            sp.wait_ge(prep_step, PREP_STEPS)

            def store_logs(p, job, n, stack, row):
                wait_emptied(sp, p, job)
                sp.dma_start(stack[row:row + PARTS, :, 0:2 * P], log_rows[:]).then_inc(log_stacked, 16)
                sp.dma_start(stack[row:row + PARTS, :, 2 * P:SP], log_rest[:]).then_inc(log_stacked, 16)

            def one_pass(p):
                if p.front is not None:
                    if p.mid is not None:
                        sp.wait_ge(work_full[BANK["E_1"]], p.uses_last_pass("E_1"))
                    sp.dma_start(x_sb[:], x[p.front]).then_inc(x_in, 16)
                if p.mid is not None:
                    store_logs(p, "L", 0, q_stack, L_ROW)
                if p.front is not None:
                    if p.mid is not None:
                        sp.wait_ge(next_ready, 4 * p.mid + 4)
                    sp.dma_start(h_sb[CLS_ROW + 1:P, 1, :],
                                 txt[p.front, 0:P - CLS_ROW - 1, :]).then_inc(txt_in, 16)
                    sp.dma_start(h_sb[0:REST, 2, :],
                                 txt[p.front, P - CLS_ROW - 1:NTXT, :]).then_inc(txt_in, 16)
                if p.back is not None:
                    wait_emptied(sp, p, "O_2")
                    sp.dma_start(out[p.back, 0:2 * P, :].rearrange("(c p) e -> p c e", p=P),
                                 out_sb[:, 0:2, :]).then_inc(out_stored, 16)
                    sp.dma_start(out[p.back, 2 * P:S, :], out_sb[0:REST, 2, :]).then_inc(out_stored, 16)
                if p.mid is not None:
                    store_logs(p, "M", 1, k_stack, M_ROW)
                if p.front is not None:
                    if p.mid is not None:
                        wait_scores(sp, p.mid, 3 * TILES - 1)
                    for t, (stack, blocks) in enumerate(((q_stack, Q_BLOCKS), (k_stack, K_BLOCKS))):
                        sp.wait_ge(parts_ready, 4 * p.front + 2 * t + 2)
                        for i, part in enumerate(blocks):
                            sp.dma_start(stack[D * i:D * i + D, :, :],
                                         qk_parts[:, t, part, :, :]).then_inc(stacked, 16)

            run_passes(sp, B, one_pass)
            sp.wait_ge(out_stored, 32 * B + OUT_FREE)

        @block.gpsimd
        def _(pool):
            count = [0]

            def prep(ins):
                count[0] += 1
                ins.then_inc(pool_prep, 1)

            def after():
                pool.wait_ge(pool_prep, count[0])

            prep(pool.memset(wo_sb[:], 0.0))
            prep(pool.memset(ident[:], 0.0))
            prep(pool.memset(mask12[:], 1.0))
            prep(pool.memset(below[:], 1.0))
            prep(pool.memset(minus_half[:], -0.5))
            after()
            prep(pool.affine_select(out=ident[:], in_=ident[:], compare_op=ALU.not_equal, fill=1.0,
                                    base=0, pattern=[[-1, P]], channel_multiplier=1))
            prep(pool.affine_select(out=mask12[:, 8:12], in_=mask12[:, 8:12], compare_op=ALU.is_ge,
                                    fill=0.0, base=0, pattern=[[-32, 4]], channel_multiplier=1))
            after()
            prep(pool.affine_select(out=mask12[:, 8:12], in_=mask12[:, 8:12], compare_op=ALU.is_ge,
                                    fill=0.0, base=REST - 1, pattern=[[32, 4]], channel_multiplier=-1))
            for i, e in enumerate(EMBED_CHOICES):
                for j, r in enumerate(RATIO_CHOICES):
                    m = below[:, 3 * i + j, :]
                    prep(pool.affine_select(out=m, in_=m, compare_op=ALU.is_ge, fill=0.0,
                                            base=r * e - 1, pattern=[[-P, HC]], channel_multiplier=-1))
            for t in (hnT, qk_parts, v_w):
                prep(pool.memset(t[:], 0.0))
            for t in (sums, a_row, mv_f, mv_b, mv_c, hbo_next, hlb_next):
                prep(pool.memset(t[:], 1.0))
            assert count[0] == POOL_PREPS, count[0]

            def rstd(which, mv, out_, n):
                pool.wait_ge(var_ready[which], n + 1)
                nc.gpsimd.tensor_tensor(out_[:], mv[:, :, 1], minus_half[:], ALU.pow)\
                    .then_inc(rstd_ready[which], 1)

            def one_pass(p):
                if p.back is not None:
                    rstd("b", mv_b, rstd_b, p.back)
                    pool.wait_ge(h2_ready, p.back + 1)
                    for c, rows in WIDE:
                        nc.gpsimd.tensor_tensor(h2b_sb[0:rows, c, :], h2_sb[0:rows, c, :],
                                                spread(b1_sb, rows, c.stop - c.start),
                                                ALU.add).then_inc(h2b_ready, 1)
                    rstd("c", mv_c, rstd_c, p.back)
                if p.mid is not None:
                    if p.back is not None:
                        pool.wait_ge(v_weighted, 3 * p.back + 3)
                    pool.wait_ge(v_ready, p.mid + 1)
                    pool.wait_ge(next_ready, 4 * p.mid + 4)
                    nc.gpsimd.tensor_tensor(pool_fence[:], pad_one[:], pad_one[:], ALU.add)
                    for dst, src in ((hbo_cur, hbo_next), (hlb_cur, hlb_next), (v_cur, v_sb)):
                        nc.gpsimd.tensor_copy(dst[:], src[:]).then_inc(cur_ready, 1)
                if p.front is not None:
                    rstd("f", mv_f, rstd_f, p.front)
                    pool.wait_ge(hn_ready, p.front + 1)
                    if p.mid is not None:
                        pool.wait_ge(cur_ready, 3 * p.mid + 3)
                    for dst, src, bias in ((hbo_next, hn_sb, bo_sb), (hlb_next, h_sb, ln_b_sb)):
                        for c, rows in WIDE:
                            nc.gpsimd.tensor_tensor(dst[0:rows, c, :], src[0:rows, c, :],
                                                    spread(bias, rows, c.stop - c.start),
                                                    ALU.add).then_inc(next_ready, 1)

            pool.wait_ge(weights_in, 16 * WEIGHT_DMAS)
            pool.wait_ge(prep_step, PREP_STEPS)
            run_passes(pool, B, one_pass)

        @block.tensor
        def _(pe):
            def work_bank(p, job, *inputs):
                wait(pe, work_free[BANK[job]], p.uses_before(job))
                wait_emptied(pe, p, *(n for n in inputs if BANK[n] != BANK[job]))
                return work[BANK[job]]

            def done(job, last):
                last.then_inc(work_full[BANK[job]], 1)

            def score_tiles(p, which, lo, hi):
                if p.mid is None:
                    return
                for k in range(lo, hi):
                    if k == 0 and which == 0:
                        pe.wait_ge(stacked, 16 * 2 * NBLK * (p.mid + 1))
                    elif k == 0:
                        pe.wait_ge(log_stacked, 32 * (2 * p.mid + which))
                    slot = TILES * which + k
                    r = slot % RING
                    wait(pe, score_free[r], p.mid * RING_USES[r] + slot // RING)
                    rows = (L_ROW, M_ROW, STACK)[which]
                    still, move = (k_stack, q_stack) if which == 1 else (q_stack, k_stack)
                    g, h, c = tile_of(k)
                    if h is None:
                        for j in range(4):
                            last = nc.tensor.matmul(score[r][32 * j:32 * j + 32, 0:S],
                                                    still[0:rows, 4 * g + j, 2 * P:SP],
                                                    move[0:rows, 4 * g + j, 0:S], start=True, stop=True)
                    else:
                        last = nc.tensor.matmul(score[r][:, 0:S], still[0:rows, h, P * c:P * c + P],
                                                move[0:rows, h, 0:S], start=True, stop=True)
                    last.then_inc(score_full[r], 1)

            def four_heads(p, job, g, matrix, weights, *inputs):
                bank = work_bank(p, job, *inputs)
                for i in range(12):
                    c, j = divmod(i, 4)
                    k = 9 * g + (8 if c == 2 else 2 * j + c)
                    last = nc.tensor.matmul(bank[32 * j:32 * j + 32, 0:S], weights(i),
                                            matrix[:, k, :], start=(c == 0), stop=(c == 2))
                done(job, last)

            def half_sum(p, job, g, matrix, weights, *inputs):
                four_heads(p, job, g, matrix,
                           lambda i: weights[:, g, i:i + 1].to_broadcast([P, 32]), *inputs)

            def turn(p, job, g, rows, *inputs):
                bank = work_bank(p, job, *inputs)
                for c in range(2):
                    nc.tensor.transpose(bank[:, P * c:P * c + P], rows[:, g, P * c:P * c + P], ident[:])
                for j in range(4):
                    last = nc.tensor.matmul(bank[32 * j:32 * j + 32, 2 * P:3 * P:32],
                                            rows[:, g, 2 * P:SP], ident[:, 0:P:32], start=True, stop=True)
                done(job, last)

            def h4(p, g):
                if p.mid is not None:
                    pe.wait_ge(first_weights, 3 * p.mid + g + 1)
                    half_sum(p, f"H4_{g}", g, PL, w_a)

            def t4(p, g):
                if p.back is not None:
                    if BANK[f"H4_{g}"] != BANK[f"T4_{g}"]:
                        pe.wait_ge(work_free[BANK[f"H4_{g}"]], p.uses_last_pass(f"H4_{g}"))
                    turn(p, f"T4_{g}", g, sums)

            def h5(p, g):
                if p.back is not None:
                    pe.wait_ge(half_weights, 3 * p.back + g + 1)
                    half_sum(p, f"H5_{g}", g, G, w_b)

            def t5(p, g):
                if p.back is not None:
                    pe.wait_ge(a_row_ready, 3 * p.back + g + 1)
                    turn(p, f"T5_{g}", g, a_row)

            def h6(p, g):
                if p.back is not None:
                    half_sum(p, f"H6_{g}", g, PL, w_a2, f"T5_{g}")

            def t6(p, g):
                if p.back is not None:
                    turn(p, f"T6_{g}", g, sums, f"H6_{g}")

            def context(p, g):
                if p.back is not None:
                    pe.wait_ge(v_weighted, 3 * p.back + g + 1)
                    four_heads(p, f"C_{g}", g, G, lambda i: v_w[:, g, i, :])

            def turn_logs(p, job, n):
                if p.mid is None:
                    return
                pe.wait_ge(log_ready, 2 * p.mid + n + 1)
                bank = work_bank(p, job)[:, :].bitcast(BF16)
                n = PARTS * H
                nc.tensor.transpose(bank[0:PARTS * GROUPS, 2 * P:3 * P],
                                    log_parts[:, 2 * n:PARTS * TILES], ident_bf[:])
                for c in range(2):
                    last = nc.tensor.transpose(bank[0:n, P * c:P * c + P],
                                               log_parts[:, n * c:n * c + n], ident_bf[:])
                done(job, last)

            def out_proj(p, t):
                if p.back is None:
                    return
                job = f"W_{t}"
                bank = work_bank(p, job, *(f"C_{g}" for g in range(GROUPS)))
                for g in range(GROUPS):
                    last = nc.tensor.matmul(bank[0:ROWS[t], 0:E], ctxT[:, g, P * t:P * t + ROWS[t]],
                                            wo_sb[:, g, :], start=(g == 0), stop=(g == GROUPS - 1))
                done(job, last)

            def turn_tokens(p, job, half, src):
                bank = work_bank(p, job)
                for t in range(3):
                    last = nc.tensor.transpose(bank[0:HALF, P * t:P * t + ROWS[t]],
                                               src[0:ROWS[t], t, HALF * half:HALF * half + HALF],
                                               ident[0:ROWS[t], 0:ROWS[t]])
                done(job, last)

            def turn_h2(p, half):
                if p.back is not None:
                    pe.wait_ge(h2n_ready, p.back + 1)
                    turn_tokens(p, f"X_{half}", half, h2n_sb)

            def ffn_up(p, c):
                if p.back is None:
                    return
                job = f"G_{c}"
                bank = work_bank(p, job, "X_0", "X_1")
                for half in range(2):
                    last = nc.tensor.matmul(bank[:, 0:S], w0_sb[:, half, P * c:P * c + P],
                                            h2T[:, half, :], start=(half == 0), stop=(half == 1))
                done(job, last)

            def ffn_down(p, t):
                if p.back is None:
                    return
                job = f"O_{t}"
                bank = work_bank(p, job, *(f"G_{c}" for c in range(HC)))
                for c in range(HC):
                    last = nc.tensor.matmul(bank[0:ROWS[t], 0:E], gT[:, c, P * t:P * t + ROWS[t]],
                                            w1_sb[:, c, :], start=(c == 0), stop=(c == HC - 1))
                done(job, last)

            def embed(p, t):
                if p.front is None:
                    return
                if t == 0:
                    pe.wait_ge(x_in, 16 * (p.front + 1))
                job = f"E_{t}"
                bank = work_bank(p, job)
                rows = (P, NPATCH - P)[t]
                for c in range(KC):
                    last = nc.tensor.matmul(bank[0:rows, 0:E], x_sb[:, c, P * t:P * t + rows],
                                            tok_w_sb[:, c, :], start=(c == 0), stop=(c == KC - 1))
                done(job, last)

            def turn_hn(p, half):
                if p.front is not None:
                    pe.wait_ge(hn_ready, p.front + 1)
                    turn_tokens(p, f"N_{half}", half, hn_sb)

            def project(p, name, m, w):
                if p.front is None:
                    return
                job = f"{name}_{m}"
                bank = work_bank(p, job, "N_0", "N_1")
                for half in range(2):
                    last = nc.tensor.matmul(bank[0:HALF, 0:S], w[:, half, m, :], hnT[:, half, 0:S],
                                            start=(half == 0), stop=(half == 1))
                done(job, last)

            def values(p, t):
                if p.front is None:
                    return
                job = f"V_{t}"
                bank = work_bank(p, job, "N_0", "N_1")
                for half in range(2):
                    if t < 2:
                        last = nc.tensor.matmul(bank[:, 0:E], hnT[:, half, P * t:P * t + P],
                                                wv_sb[:, half, :], start=(half == 0), stop=(half == 1))
                        continue
                    for j in range(4):
                        last = nc.tensor.matmul(bank[32 * j:32 * j + 32, 0:E], hnT[:, half, 2 * P:SP],
                                                wv_sb[:, half, :], start=(half == 0), stop=(half == 1))
                done(job, last)

            def one_pass(p):
                t4(p, 0)
                t4(p, 1)
                h5(p, 0)
                t4(p, 2)
                score_tiles(p, 0, 0, 2)
                h5(p, 1)
                t5(p, 0)
                score_tiles(p, 0, 2, 6)
                h5(p, 2)
                t5(p, 1)
                score_tiles(p, 0, 6, 10)
                h6(p, 0)
                t5(p, 2)
                score_tiles(p, 0, 10, 15)
                h6(p, 1)
                t6(p, 0)
                score_tiles(p, 0, 15, 21)
                h6(p, 2)
                t6(p, 1)
                score_tiles(p, 0, 21, TILES)
                context(p, 0)
                t6(p, 2)
                context(p, 1)
                turn_logs(p, "L", 0)
                context(p, 2)
                out_proj(p, 0)
                out_proj(p, 1)
                out_proj(p, 2)
                score_tiles(p, 1, 0, 4)
                embed(p, 0)
                score_tiles(p, 1, 4, 9)
                embed(p, 1)
                score_tiles(p, 1, 9, 13)
                turn_h2(p, 0)
                turn_h2(p, 1)
                score_tiles(p, 1, 13, 17)
                ffn_up(p, 0)
                score_tiles(p, 1, 17, 20)
                ffn_up(p, 1)
                score_tiles(p, 1, 20, 23)
                ffn_up(p, 2)
                score_tiles(p, 1, 23, TILES)
                ffn_up(p, 3)
                ffn_up(p, 4)
                ffn_up(p, 5)
                turn_hn(p, 0)
                turn_hn(p, 1)
                ffn_down(p, 0)
                turn_logs(p, "M", 1)
                ffn_down(p, 1)
                ffn_down(p, 2)
                project(p, "Q", 0, wq_sb)
                score_tiles(p, 2, 0, 5)
                project(p, "Q", 1, wq_sb)
                score_tiles(p, 2, 5, 10)
                project(p, "K", 0, wk_sb)
                score_tiles(p, 2, 10, 15)
                project(p, "K", 1, wk_sb)
                score_tiles(p, 2, 15, 20)
                values(p, 0)
                score_tiles(p, 2, 20, 23)
                values(p, 1)
                h4(p, 0)
                score_tiles(p, 2, 23, TILES)
                values(p, 2)
                h4(p, 1)
                h4(p, 2)

            pe.wait_ge(prep_step, PREP_STEPS)
            run_passes(pe, B, one_pass)

        @block.scalar
        def _(act):
            def exp_tiles(p, which, lo, hi):
                if p.mid is None:
                    return
                for k in range(lo, hi):
                    slot = TILES * which + k
                    col = column_of(k)
                    if which < 2:
                        act.wait_ge(max_ready, 2 * TILES * p.mid + slot + 1)
                    else:
                        wait_scores(act, p.mid, slot)
                    neg, total, dst = ((neg_r, rho, junk[:, slot % RING, :]), (neg_c, kappa, G[:, k, :]),
                                       (None, sigma, PL[:, k, :]))[which]
                    bias = {} if neg is None else {"bias": neg[:, col:col + 1]}
                    nc.scalar.activation(dst, score[slot % RING][:, 0:S], ACT.Exp,
                                         accum_out=total[:, col:col + 1],
                                         **bias).then_inc(score_free[slot % RING], 1)

            def log_sums(p, n):
                if p.mid is not None:
                    wait_exp(act, p.mid, TILES * (n + 1) - 1)
                    nc.scalar.activation(ln_sum[:], (rho, kappa)[n][:], ACT.Ln).then_inc(ln_ready, 1)

            def a_rows(p, g):
                if p.back is None:
                    return
                job = f"H5_{g}"
                bank = wait_full(act, p, job)
                nc.scalar.activation(ln_row[:, g, :], bank[:, 0:S], ACT.Ln)\
                    .then_inc(work_free[BANK[job]], 1)
                wait_emptied(act, p, job)
                nc.scalar.activation(a_row[:, g, 0:S], ln_row[:, g, :], ACT.Exp, scale=-1.0)\
                    .then_inc(a_row_ready, 1)

            def copy_out(p, job, dst):
                if p.active(job):
                    bank = wait_full(act, p, job)
                    nc.scalar.activation(dst, bank[0:dst.shape[0], 0:S], ACT.Copy)\
                        .then_inc(work_free[BANK[job]], 1)

            def gelu(p, c):
                if p.back is None:
                    return
                job = f"G_{c}"
                bank = wait_full(act, p, job)
                nc.scalar.activation(gT[:, c, :], bank[:, 0:S], ACT.Gelu_apprx_tanh,
                                     bias=b0_sb[:, c:c + 1]).then_inc(work_free[BANK[job]], 1)
                if c == HC - 1:
                    act.preload_act_table_set("natural_log_exp_and_others")

            def one_pass(p):
                a_rows(p, 0)
                exp_tiles(p, 0, 0, 2)
                a_rows(p, 1)
                exp_tiles(p, 0, 2, 6)
                a_rows(p, 2)
                exp_tiles(p, 0, 6, 10)
                copy_out(p, "H6_0", sums[:, 0, 0:S])
                exp_tiles(p, 0, 10, 15)
                copy_out(p, "H6_1", sums[:, 1, 0:S])
                exp_tiles(p, 0, 15, 21)
                copy_out(p, "H6_2", sums[:, 2, 0:S])
                exp_tiles(p, 0, 21, TILES)
                log_sums(p, 0)
                exp_tiles(p, 1, 0, 13)
                copy_out(p, "X_0", h2T[:, 0, :])
                copy_out(p, "X_1", h2T[:, 1, :])
                exp_tiles(p, 1, 13, TILES)
                log_sums(p, 1)
                gelu(p, 0)
                gelu(p, 1)
                gelu(p, 2)
                gelu(p, 3)
                gelu(p, 4)
                gelu(p, 5)
                copy_out(p, "N_0", hnT[:, 0, 0:S])
                copy_out(p, "N_1", hnT[:, 1, 0:S])
                exp_tiles(p, 2, 0, 26)
                copy_out(p, "H4_0", sums[:, 0, 0:S])
                exp_tiles(p, 2, 26, TILES)
                copy_out(p, "H4_1", sums[:, 1, 0:S])
                copy_out(p, "H4_2", sums[:, 2, 0:S])

            act.preload_act_table_set("natural_log_exp_and_others")
            act.wait_ge(prep_step, PREP_STEPS)
            run_passes(act, B, one_pass)

        @block.vector
        def _(dve):
            count = [0]

            def prep(ins):
                count[0] += 1
                ins.then_inc(prep_step, 1)
                dve.wait_ge(prep_step, count[0])

            dve.wait_ge(weights_in, 16 * WEIGHT_DMAS)
            dve.wait_ge(pool_prep, POOL_PREPS)
            prep(nc.vector.tensor_copy(ident_bf[:], ident[:]))
            prep(nc.vector.memset(q_stack[L_ROW:STACK, :, :], 1.0))
            prep(nc.vector.memset(k_stack[L_ROW:STACK, :, :], 1.0))
            prep(nc.vector.reduce_sum(mask_rest[:], mask12[:, 8:12], AX_X))
            prep(nc.vector.tensor_scalar(pad_one[:], mask_rest[:], -1.0, 1.0, ALU.mult, ALU.add))
            prep(nc.vector.tensor_scalar(pad_neg[:], pad_one[:], NEG, None, ALU.mult))
            for i in range(3):
                prep(nc.vector.tensor_scalar(pair[:, 3 * i:3 * i + 3], alpha_sb[:, 3:6],
                                             alpha_sb[:, i:i + 1], None, ALU.mult))
            prep(nc.vector.memset(coef[:], 0.0))
            for i in (2, 1, 0):
                for j in range(3):
                    acc = coef[:, i + 1, :] if j == 0 and i < 2 else coef[:, i, :]
                    n = 3 * i + j
                    prep(nc.vector.scalar_tensor_tensor(out=coef[:, i, :], in0=below[:, n, :],
                                                        scalar=pair[:, n:n + 1], in1=acc,
                                                        op0=ALU.mult, op1=ALU.add))
            prep(nc.vector.tensor_tensor(b0_sb[:], b0_sb[:], coef[:, 0, :], ALU.mult))
            lo = 0
            for i, e in enumerate(EMBED_CHOICES):
                prep(nc.vector.tensor_tensor(w1_sb[:, :, lo:e], w1_sb[:, :, lo:e],
                                             coef[:, i, :].unsqueeze(2).to_broadcast([P, HC, e - lo]),
                                             ALU.mult))
                prep(nc.vector.reduce_sum(coef_out[:, i:i + 1], pair[:, 3 * i:9], AX_X))
                prep(nc.vector.tensor_scalar(b1_sb[:, lo:e], b1_sb[:, lo:e], coef_out[:, i:i + 1], None,
                                             ALU.mult))
                lo = e
            prep(nc.vector.memset(coef_row[:], 0.0))
            for i, e in enumerate(EMBED_CHOICES):
                for j, r in enumerate(RATIO_CHOICES):
                    for half in range(2):
                        rows = min(max(e - HALF * half, 0), HALF)
                        if rows:
                            c = coef_row[0:rows, half, 0:r * e]
                            n = 3 * i + j
                            prep(nc.vector.tensor_scalar(c, c, pair[0:rows, n:n + 1], None, ALU.add))
            prep(nc.vector.tensor_tensor(w0_sb[:], w0_sb[:], coef_row[:], ALU.mult))
            assert count[0] == PREP_STEPS, count[0]

            nc.vector.memset(fence[:], 0.0).then_inc(out_stored, OUT_FREE)
            steps = {}

            def step(p, stage, ins):
                steps[stage] += 1
                ins.then_inc(vector_step[stage], 1)
                dve.wait_ge(vector_step[stage], p.images[stage] * LINKS[stage] + steps[stage])

            def max_tiles(p, which, lo, hi):
                if p.mid is None:
                    return
                for k in range(lo, hi):
                    slot = TILES * which + k
                    col = column_of(k)
                    wait_scores(dve, p.mid, slot)
                    nc.vector.tensor_reduce((neg_r, neg_c)[which][:, col:col + 1],
                                            score[slot % RING][:, 0:S], op=ALU.max, axis=AX_X,
                                            negate=True).then_inc(max_ready, 1)

            def logs(p, n):
                if p.mid is None:
                    return
                dve.wait_ge(ln_ready, 2 * p.mid + n + 1)
                step(p, "mid", nc.vector.tensor_tensor(log_f[:], (neg_r, neg_c)[n][:], ln_sum[:],
                                                       ALU.subtract))
                if n == 0:
                    f = log_f[:, 2 * H:TILES]
                    step(p, "mid", nc.vector.tensor_scalar(f, f, mask_rest[:], pad_neg[:],
                                                           ALU.mult, ALU.add))
                def whole(t):
                    return t[:, 0:2 * H].rearrange("p (c h) -> p c h", c=2)

                def rest(t):
                    return t[:, 2 * H:TILES]

                split_at = 2 * PARTS * H
                parts = [(log_parts[:, 0:split_at].rearrange("p (c n h) -> p c n h", c=2, n=PARTS)[:, :, i, :],
                          log_parts[:, split_at + GROUPS * i:split_at + GROUPS * i + GROUPS])
                         for i in range(PARTS)]
                both = (whole, rest)
                for i, view in enumerate(both):
                    last = nc.vector.tensor_copy(parts[0][i], view(log_f))
                step(p, "mid", last)
                for i, view in enumerate(both):
                    last = nc.vector.tensor_tensor(view(log_r), view(log_f), parts[0][i], ALU.subtract)
                step(p, "mid", last)
                for i, view in enumerate(both):
                    last = nc.vector.tensor_copy(parts[1][i], view(log_r))
                step(p, "mid", last)
                for i, view in enumerate(both):
                    last = nc.vector.tensor_tensor(parts[2][i], view(log_r), parts[1][i], ALU.subtract)
                last.then_inc(log_ready, 1)

            def log_rows_out(p, job, n):
                if p.mid is None:
                    return
                wait(dve, log_stacked, 32 * (2 * p.mid + n))
                bank = wait_full(dve, p, job)[:, :].bitcast(BF16)
                nc.vector.tensor_copy(log_rows[:], bank[0:PARTS * H, 0:2 * P])
                nc.vector.tensor_copy(log_rest[:], bank[0:PARTS * GROUPS, 2 * P:3 * P])\
                    .then_inc(work_free[BANK[job]], 1)

            def by_head(t, g):
                return t[:, 0:2 * H].rearrange("p (c h) -> p c h", c=2)[:, :, 4 * g:4 * g + 4]

            def kappa_weights(p):
                if p.mid is None:
                    return
                step(p, "mid", nc.vector.reciprocal(rest_tmp[:], kappa[:, 2 * H:TILES]))
                for g in range(GROUPS):
                    nc.vector.reciprocal(inv_kappa[:, g, 0:8].rearrange("p (c j) -> p c j", c=2),
                                         by_head(kappa, g))
                nc.vector.tensor_tensor(inv_kappa[:, :, 8:12],
                                        rest_tmp[:].unsqueeze(2).to_broadcast([P, GROUPS, 4]),
                                        mask12[:, 8:12].unsqueeze(1).to_broadcast([P, GROUPS, 4]),
                                        ALU.mult).then_inc(kappa_ready, 1)

            def first_half_weights(p, g):
                if p.mid is None:
                    return
                wait_exp(dve, p.mid, 2 * TILES + 9 * g + 8)
                nc.vector.reciprocal(w_a[:, g, 0:8].rearrange("p (c j) -> p c j", c=2),
                                     by_head(sigma, g))
                rest = sigma_rest[:, g:g + 1]
                step(p, "mid", nc.vector.tensor_scalar(rest, sigma[:, 2 * H + g:2 * H + g + 1],
                                                        pad_one[:], None, ALU.add))
                step(p, "mid", nc.vector.reciprocal(rest, rest))
                nc.vector.tensor_scalar(w_a[:, g, 8:12], mask12[:, 8:12], rest, None, ALU.mult)\
                    .then_inc(first_weights, 1)

            def turned(p, job):
                bank = wait_full(dve, p, job)
                return bank[:, 0:3 * P].rearrange("p (c j r) -> p c j r", c=3, r=32)[:, :, :, 0]

            def three(t, g):
                return t[:, g, :].rearrange("p (c j) -> p c j", c=3)

            def t4(p, g):
                if p.back is None:
                    return
                job = f"T4_{g}"
                nc.vector.reciprocal(three(recip12, g), turned(p, job)).then_inc(work_free[BANK[job]], 1)
                wait_emptied(dve, p, job)
                if g == 0:
                    dve.wait_ge(kappa_ready, p.back + 1)
                nc.vector.tensor_tensor(w_b[:, g, :], recip12[:, g, :], inv_kappa[:, g, :],
                                        ALU.mult).then_inc(half_weights, 1)

            def t5(p, g):
                if p.back is not None:
                    job = f"T5_{g}"
                    nc.vector.tensor_tensor(three(w_a2, g), turned(p, job),
                                            mask12[:].rearrange("p (c j) -> p c j", c=3),
                                            ALU.mult).then_inc(work_free[BANK[job]], 1)

            def t6(p, g):
                if p.back is None:
                    return
                job = f"T6_{g}"
                nc.vector.reciprocal(three(recip12, g), turned(p, job)).then_inc(work_free[BANK[job]], 1)
                wait_emptied(dve, p, job)
                step(p, "back", nc.vector.tensor_tensor(w_b2[:, g, :], recip12[:, g, :],
                                                        inv_kappa[:, g, :], ALU.mult))
                if g == 0:
                    dve.wait_ge(cur_ready, 3 * p.back + 3)
                heads = v_cur[:, :, 4 * D * g:4 * D * g + 4 * D]
                nc.vector.tensor_tensor(
                    v_w[:, g, :, 0:D].rearrange("p (c j) d -> p c j d", c=3),
                    heads.rearrange("p c (j d) -> p c j d", j=4),
                    three(w_b2, g).unsqueeze(3).to_broadcast([P, 3, 4, D]),
                    ALU.mult).then_inc(v_weighted, 1)

            def context(p, g):
                if p.back is None:
                    return
                job = f"C_{g}"
                dve.wait_ge(a_row_ready, 3 * p.back + g + 1)
                bank = wait_full(dve, p, job)
                nc.vector.tensor_tensor(ctxT[:, g, :], bank[:, 0:S], a_row[:, g, 0:S], ALU.mult)\
                    .then_inc(work_free[BANK[job]], 1)

            def statistics(p, stage, src, stats, mv, eps, ready):
                for t in range(3):
                    last = nc.vector.bn_stats(stats[0:ROWS[t], t, :], src[0:ROWS[t], t, :])
                step(p, stage, last)
                nc.vector.memset(fence[:], 0.0)
                for t in range(3):
                    last = nc.vector.bn_aggr(mv[0:ROWS[t], t, :], stats[0:ROWS[t], t, :])
                step(p, stage, last)
                nc.vector.tensor_scalar(mv[:, :, 1], mv[:, :, 1], eps, None, ALU.add)\
                    .then_inc(ready, 1)

            def output_tokens(p, t):
                if p.back is None:
                    return
                job = f"W_{t}"
                bank = wait_full(dve, p, job)
                rows = ROWS[t]
                nc.vector.tensor_tensor(y_sb[0:rows, t, :], bank[0:rows, 0:E],
                                        hbo_cur[0:rows, t, :], ALU.add)\
                    .then_inc(work_free[BANK[job]], 1)

            def output_statistics(p):
                if p.back is not None:
                    wait_emptied(dve, p, "W_0", "W_1", "W_2")
                    statistics(p, "back", y_sb, stats_b, mv_b, ATTN_EPS, var_ready["b"])

            def residual(p):
                if p.back is None:
                    return
                dve.wait_ge(rstd_ready["b"], p.back + 1)
                for t in range(3):
                    rows = ROWS[t]
                    last = nc.vector.scalar_tensor_tensor(
                        out=y_sb[0:rows, t, :], in0=y_sb[0:rows, t, :], scalar=mv_b[0:rows, t, 0:1],
                        in1=ln_g_sb[0:rows, :], op0=ALU.subtract, op1=ALU.mult)
                step(p, "back", last)
                for t in range(3):
                    rows = ROWS[t]
                    last = nc.vector.scalar_tensor_tensor(
                        out=h2_sb[0:rows, t, :], in0=y_sb[0:rows, t, :], scalar=rstd_b[0:rows, t:t + 1],
                        in1=hlb_cur[0:rows, t, :], op0=ALU.mult, op1=ALU.add)
                last.then_inc(h2_ready, 1)

            def residual_statistics(p):
                if p.back is not None:
                    dve.wait_ge(h2_ready, p.back + 1)
                    statistics(p, "back", h2_sb, stats_c, mv_c, LN_EPS, var_ready["c"])

            def normalise(p, image, src, dst, mv, rstd, which, ready):
                dve.wait_ge(rstd_ready[which], image + 1)
                for t in range(3):
                    rows = ROWS[t]
                    last = nc.vector.tensor_scalar(dst[0:rows, t, :], src[0:rows, t, :],
                                                   mv[0:rows, t, 0:1], rstd[0:rows, t:t + 1],
                                                   ALU.subtract, ALU.mult)
                last.then_inc(ready, 1)

            def ffn_out(p, t):
                if p.back is None:
                    return
                job = f"O_{t}"
                if t == 0:
                    dve.wait_ge(h2b_ready, 2 * p.back + 2)
                    dve.wait_ge(out_stored, 32 * p.back + OUT_FREE)
                bank = wait_full(dve, p, job)
                rows = ROWS[t]
                nc.vector.tensor_tensor(out_sb[0:rows, t, :], bank[0:rows, 0:E], h2b_sb[0:rows, t, :],
                                        ALU.add).then_inc(work_free[BANK[job]], 1)

            def embed(p, t):
                if p.front is None:
                    return
                if t == 0 and p.mid is not None:
                    dve.wait_ge(next_ready, 4 * p.mid + 4)
                job = f"E_{t}"
                bank = wait_full(dve, p, job)
                rows = (P, NPATCH - P)[t]
                nc.vector.tensor_tensor(h_sb[0:rows, t, :], bank[0:rows, 0:E], tok_b_sb[0:rows, :],
                                        ALU.add).then_inc(work_free[BANK[job]], 1)

            def embed_statistics(p):
                if p.front is None:
                    return
                wait_emptied(dve, p, "E_0", "E_1")
                dve.wait_ge(txt_in, 32 * (p.front + 1))
                statistics(p, "front", h_sb, stats_f, mv_f, LN_EPS, var_ready["f"])

            def split(p, name, m, bias, scale):
                if p.front is None:
                    return
                job = f"{name}_{m}"
                i = 2 * (name == "K") + m
                bank = wait_full(dve, p, job)
                nc.vector.tensor_scalar(qk_f[:, i, 0:S], bank[0:HALF, 0:S], bias[:, m:m + 1], scale,
                                        ALU.add, ALU.mult).then_inc(work_free[BANK[job]], 1)
                wait_emptied(dve, p, job)
                if i == 0:
                    wait(dve, stacked, 16 * 2 * NBLK * p.front)
                part = [qk_parts[:, i // 2, n, m, 0:S] for n in range(PARTS)]
                step(p, "front", nc.vector.tensor_copy(part[0], qk_f[:, i, 0:S]))
                step(p, "front", nc.vector.tensor_tensor(qk_r[:, i, 0:S], qk_f[:, i, 0:S], part[0],
                                                         ALU.subtract))
                step(p, "front", nc.vector.tensor_copy(part[1], qk_r[:, i, 0:S]))
                nc.vector.tensor_tensor(part[2], qk_r[:, i, 0:S], part[1], ALU.subtract)\
                    .then_inc(parts_ready, 1)

            def values(p, t):
                if p.front is None:
                    return
                if t == 0 and p.mid is not None:
                    dve.wait_ge(cur_ready, 3 * p.mid + 3)
                job = f"V_{t}"
                bank = wait_full(dve, p, job)
                nc.vector.tensor_tensor(v_sb[:, t, :], bank[:, 0:E], bv_sb[:], ALU.add)\
                    .then_inc(work_free[BANK[job]], 1)
                if t == 2:
                    wait_emptied(dve, p, "V_0", "V_1", "V_2")
                    nc.vector.memset(fence[:], 0.0).then_inc(v_ready, 1)

            def one_pass(p):
                steps.update(dict.fromkeys(LINKS, 0))
                t4(p, 0)
                t4(p, 1)
                t4(p, 2)
                max_tiles(p, 0, 0, 2)
                t5(p, 0)
                max_tiles(p, 0, 2, 6)
                t5(p, 1)
                max_tiles(p, 0, 6, 10)
                t5(p, 2)
                max_tiles(p, 0, 10, 15)
                t6(p, 0)
                max_tiles(p, 0, 15, 21)
                t6(p, 1)
                max_tiles(p, 0, 21, TILES)
                context(p, 0)
                logs(p, 0)
                t6(p, 2)
                context(p, 1)
                log_rows_out(p, "L", 0)
                context(p, 2)
                output_tokens(p, 0)
                output_tokens(p, 1)
                output_tokens(p, 2)
                output_statistics(p)
                max_tiles(p, 1, 0, 4)
                residual(p)
                max_tiles(p, 1, 4, 6)
                residual_statistics(p)
                max_tiles(p, 1, 6, 8)
                embed(p, 0)
                max_tiles(p, 1, 8, 10)
                embed(p, 1)
                if p.back is not None:
                    normalise(p, p.back, h2_sb, h2n_sb, mv_c, rstd_c, "c", h2n_ready)
                max_tiles(p, 1, 10, 14)
                embed_statistics(p)
                max_tiles(p, 1, 14, 18)
                if p.front is not None:
                    normalise(p, p.front, h_sb, hn_sb, mv_f, rstd_f, "f", hn_ready)
                max_tiles(p, 1, 18, TILES)
                logs(p, 1)
                kappa_weights(p)
                ffn_out(p, 0)
                log_rows_out(p, "M", 1)
                ffn_out(p, 1)
                ffn_out(p, 2)
                split(p, "Q", 0, bq_sb, D ** -0.5)
                split(p, "Q", 1, bq_sb, D ** -0.5)
                split(p, "K", 0, bk_sb, 1.0)
                split(p, "K", 1, bk_sb, 1.0)
                first_half_weights(p, 0)
                values(p, 0)
                first_half_weights(p, 1)
                values(p, 1)
                values(p, 2)
                first_half_weights(p, 2)
                for stage, n in steps.items():
                    assert p.images[stage] is None or n == LINKS[stage], (stage, n)

            run_passes(dve, B, one_pass)


def lay_out(inputs):
    import numpy as np

    a = {k: np.asarray(v) for k, v in inputs.items()}
    B = a["x"].shape[0]
    x = a["x"].reshape(B, 3, 14, 16, 14, 16).transpose(0, 1, 3, 5, 2, 4).reshape(B, KC, P, NPATCH)

    def halves(w):
        return w.reshape(2, HALF, -1).transpose(1, 0, 2)

    def qk(w):
        w = w.reshape(2, HALF, HH, 2, D).transpose(1, 0, 3, 4, 2)
        return w.reshape(HALF, 2, 2, HALF)

    def qk_bias(b):
        return b.reshape(HH, 2, D).transpose(2, 0, 1).reshape(HALF, 2)

    d = {
        "x": x.transpose(0, 2, 1, 3),
        "txt": a["txt"],
        "tok_w": a["L0_tok_W"].reshape(KC, P, E).transpose(1, 0, 2),
        "tok_b": a["L0_tok_b"],
        "cls": a["L0_tok_cls_token"].reshape(1, E),
        "wq": qk(a["L0_attn_Wq"]), "wk": qk(a["L0_attn_Wk"]), "wv": halves(a["L0_attn_Wv"]),
        "wo": a["L0_attn_Wo"].reshape(GROUPS, 4, D, E).transpose(1, 2, 0, 3),
        "bq": qk_bias(a["L0_attn_bq"]), "bk": qk_bias(a["L0_attn_bk"]),
        "bv": a["L0_attn_bv"], "bo": a["L0_attn_bo"],
        "ln_g": a["L0_attn_ln_g"], "ln_b": a["L0_attn_ln_b"],
        "w_fc": halves(a["L0_ffn_w_fc"].T),
        "b_fc": a["L0_ffn_b_fc"].reshape(HC, P).T,
        "w_proj": a["L0_ffn_w_proj"].T.reshape(HC, P, E).transpose(1, 0, 2),
        "b_proj": a["L0_ffn_b_proj"],
        "alpha_e": a["L0_ffn_alpha_e"], "alpha_r": a["L0_ffn_alpha_r"],
    }
    return {k: np.ascontiguousarray(v) for k, v in d.items()}


def kernel(**inputs):
    import numpy as np
    import concourse.bacc as bacc
    from concourse.bass_utils import run_bass_kernel_spmd

    nc = bacc.Bacc("TRN2", target_bir_lowering=False, num_devices=1)
    arrays = {f"in_{k}": v for k, v in lay_out(inputs).items()}
    args = {k[3:]: nc.dram_tensor(k, v.shape, mybir.dt.from_np(v.dtype), kind="ExternalInput").ap()
            for k, v in arrays.items()}
    B = arrays["in_x"].shape[0]
    out = nc.dram_tensor("out_tokens", (B, S, E), F32, kind="ExternalOutput").ap()
    early_fusion_kernel(nc, out=out, **args)
    got = np.asarray(run_bass_kernel_spmd(nc, [arrays], core_ids=[0]).results[0]["out_tokens"])
    return np.concatenate([got[:, NPATCH:NPATCH + 1], got[:, :NPATCH], got[:, NPATCH + 1:]], axis=1)
```

```python
from contextlib import ExitStack

import concourse.bass as bass
from concourse import mybir

ALU = mybir.AluOpType
ACT = mybir.ActivationFunctionType
AX_X = mybir.AxisListType.X
F32 = mybir.dt.float32
BF16 = mybir.dt.bfloat16

P = 128
E = 192
H = 12
D = E // H
S = 274
NPATCH = 196
NTXT = 77
KC = 768 // P
REST = S - 2 * P
SP = 2 * P + 32
CLS_ROW = NPATCH - P
HALF = E // 2
HH = H // 2
GROUPS = H // 4
TILES = 9 * GROUPS
HID = 768
HC = HID // P
PARTS = 3
Q_BLOCKS = (0, 0, 1, 1, 0, 2)
K_BLOCKS = (0, 1, 0, 1, 2, 0)
NBLK = len(Q_BLOCKS)
L_ROW = NBLK * D
M_ROW = L_ROW + PARTS
STACK = M_ROW + PARTS
PREP_STEPS = 46
NEG = -1.0e30
LN_EPS, ATTN_EPS = 1e-5, 1e-12
EMBED_CHOICES = (96, 144, 192)
RATIO_CHOICES = (2, 3, 4)

JOBS = (
    "G_0", "G_1", "G_2", "G_3", "G_4", "G_5", "T4_0", "T4_1", "H5_0", "T4_2", "H5_1", "T5_0",
    "H6_0", "T5_1", "H5_2", "H6_1", "T5_2", "T6_0", "T6_1", "H6_2", "C_0", "T6_2", "L", "O_0",
    "O_1", "C_1", "C_2", "W_0", "W_1", "W_2", "O_2", "M", "E_0", "E_1", "X_0", "X_1", "N_0",
    "N_1", "H4_0", "Q_0", "V_0", "Q_1", "K_0", "H4_1", "V_1", "K_1", "V_2", "H4_2"
)
NBANK = 4
STAGE_OF_KIND = {"G": "late", "O": "late", "L": "mid", "M": "mid", "H4": "mid",
                 **dict.fromkeys(("E", "N", "Q", "K", "V"), "front")}
STAGE = {n: STAGE_OF_KIND.get(n.split("_")[0], "back") for n in JOBS}
BANK = {n: i % NBANK for i, n in enumerate(JOBS)}
RING = 4
RING_USES = [len(range(r, 3 * TILES, RING)) for r in range(RING)]

LINKS = {"front": 2 + 4 * 3, "mid": 10 + 2 * GROUPS, "back": 14 - 2 * GROUPS}


def tile_of(k):
    g, i = divmod(k, 9)
    return (g, None, 2) if i == 8 else (g, 4 * g + i // 2, i % 2)


def column_of(k):
    g, h, c = tile_of(k)
    return 2 * H + g if h is None else c * H + h


class Pass:

    def __init__(self, images, banks_before, last_active=None, parity=0):
        self.back_parity = self.front_parity = parity
        self.mid_parity = 1 - parity
        self.images = images
        self.banks_before = banks_before
        self.last_active = last_active
        self.late, self.back = images["late"], images["back"]
        self.mid, self.front = images["mid"], images["front"]

    def active(self, job):
        return self.images[STAGE[job]] is not None

    def uses_before(self, job):
        mine = [n for n in JOBS if self.active(n) and BANK[n] == BANK[job]]
        return self.banks_before[BANK[job]] + mine.index(job)

    def uses_last_pass(self, job):
        later = [n for n in JOBS[JOBS.index(job) + 1:]
                 if BANK[n] == BANK[job] and self.last_active[STAGE[n]]]
        return self.banks_before[BANK[job]] - len(later)

    def uses(self):
        return [sum(self.active(n) and BANK[n] == r for n in JOBS) for r in range(NBANK)]


def images_of(it, B):
    images = {"late": it - 1, "back": it, "mid": it + 1, "front": it + 2}
    return {stage: n if 0 <= n < B else None for stage, n in images.items()}


def run_passes(engine, B, one_pass):
    before = [0] * NBANK

    def last_active(it):
        return {stage: image is not None for stage, image in images_of(it - 1, B).items()}

    def fixed(it):
        nonlocal before
        p = Pass(images_of(it, B), list(before), last_active(it), it % 2)
        one_pass(p)
        before = [a + b for a, b in zip(before, p.uses())]

    first = 2 + B % 2
    for it in range(-2, first):
        fixed(it)
    full = Pass({"late": 0, "back": 1, "mid": 2, "front": 3}, before).uses()
    with engine.Fori(0, (B - 2 - first) // 2) as turn:
        for i in range(2):
            it = 2 * turn + (first + i)
            one_pass(Pass({"late": it - 1, "back": it, "mid": it + 1, "front": it + 2},
                          [turn * (2 * n) + (a + i * n) for n, a in zip(full, before)],
                          last_active(first + i), (first + i) % 2))
    before = [a + (B - 2 - first) * n for a, n in zip(before, full)]
    for it in range(B - 2, B + 1):
        fixed(it)


def early_fusion_kernel(nc, x, txt, tok_w, tok_b, cls, wq, wk, wv, wo, bq, bk, bv, bo, ln_g, ln_b,
                        w_fc, b_fc, w_proj, b_proj, alpha_e, alpha_r, out):
    B = x.shape[0]
    with ExitStack() as ctx:
        def sb(name, shape, dt=F32):
            return ctx.enter_context(nc.sbuf_tensor(name, shape, dt))

        def sem(name):
            return ctx.enter_context(nc.semaphore(name))

        ident = sb("ident", [P, P])
        ident_bf = sb("ident_bf", [P, P], BF16)
        mask12 = sb("mask12", [P, 12])
        mask_rest = sb("mask_rest", [P, 1])
        pad_one = sb("pad_one", [P, 1])
        pad_neg = sb("pad_neg", [P, 1])
        minus_half = sb("minus_half", [P, 3])
        tok_w_sb = sb("tok_w_sb", [P, KC, E])
        wq_sb = sb("wq_sb", [HALF, 2, 2, HALF])
        wk_sb = sb("wk_sb", [HALF, 2, 2, HALF])
        wv_sb = sb("wv_sb", [HALF, 2, E])
        wo_sb = sb("wo_sb", [P, GROUPS, E])
        w0_sb = sb("w0_sb", [HALF, 2, HID])
        w1_sb = sb("w1_sb", [P, HC, E])
        bq_sb = sb("bq_sb", [HALF, 2])
        bk_sb = sb("bk_sb", [HALF, 2])
        tok_b_sb = sb("tok_b_sb", [P, E])
        bv_sb = sb("bv_sb", [P, E])
        bo_sb = sb("bo_sb", [P, E])
        ln_g_sb = sb("ln_g_sb", [P, E])
        ln_b_sb = sb("ln_b_sb", [P, E])
        b1_sb = sb("b1_sb", [P, E])
        b0_sb = sb("b0_sb", [P, HC])
        alpha_sb = sb("alpha_sb", [P, 6])
        pair = sb("pair", [P, 9])
        below = sb("below", [P, 9, HC])
        coef = sb("coef", [P, 3, HC])
        coef_out = sb("coef_out", [P, 3])
        fence = sb("fence", [P, 1])
        pool_fence = sb("pool_fence", [P, 1])

        x_sb = sb("x_sb", [P, KC, NPATCH])
        h_sb = sb("h_sb", [P, 3, E])
        hn_sb = sb("hn_sb", [P, 3, E])
        hnT = sb("hnT", [HALF, 2, SP])
        qk_f = sb("qk_f", [HALF, 4, SP])
        qk_r = sb("qk_r", [HALF, SP])
        qk_parts = sb("qk_parts", [HALF, 2, PARTS, 2, SP], BF16)
        v_sb = sb("v_sb", [P, 3, E])
        stats_f = sb("stats_f", [P, 3, 6])
        mv_f = sb("mv_f", [P, 3, 2])
        rstd_f = sb("rstd_f", [P, 3])
        q_stack = sb("q_stack", [STACK, 2, H, SP], BF16)
        k_stack = sb("k_stack", [STACK, 2, H, SP], BF16)
        neg_r = sb("neg_r", [P, TILES])
        neg_c = sb("neg_c", [P, TILES])
        rho = sb("rho", [P, TILES])
        kappa = sb("kappa", [P, TILES])
        sigma = sb("sigma", [P, TILES])
        ln_sum = sb("ln_sum", [P, TILES])
        log_f = sb("log_f", [P, TILES])
        log_r = sb("log_r", [P, TILES])
        log_parts = sb("log_parts", [P, PARTS * TILES], BF16)
        log_rows = sb("log_rows", [PARTS * H, 2 * P], BF16)
        log_rest = sb("log_rest", [PARTS * GROUPS, P], BF16)
        junk = sb("junk", [P, RING, S], BF16)
        G = sb("G", [P, TILES, S])
        PL = sb("PL", [P, TILES, S])
        rest_tmp = sb("rest_tmp", [P, GROUPS])
        sigma_rest = sb("sigma_rest", [P, GROUPS])
        inv_kappa = sb("inv_kappa", [P, GROUPS, 12])
        w_a = sb("w_a", [P, GROUPS, 12])
        w_b = sb("w_b", [P, GROUPS, 12])
        w_a2 = sb("w_a2", [P, GROUPS, 12])
        w_b2 = sb("w_b2", [P, GROUPS, 12])
        recip12 = sb("recip12", [P, GROUPS, 12])
        sums = sb("sums", [P, GROUPS, SP])
        ln_row = sb("ln_row", [P, GROUPS, S])
        a_row = sb("a_row", [P, GROUPS, SP])
        v_cur = sb("v_cur", [P, 3, E])
        v_w = sb("v_w", [P, GROUPS, 12, 32])
        ctxT = sb("ctxT", [P, GROUPS, S])
        hbo_next = sb("hbo_next", [P, 3, E])
        hlb_next = sb("hlb_next", [P, 3, E])
        hbo_cur = sb("hbo_cur", [P, 3, E])
        hlb_cur = sb("hlb_cur", [P, 3, E])
        y_sb = sb("y_sb", [P, 3, E])
        h2_sb = sb("h2_sb", [P, 3, E])
        h2b_sb = sb("h2b_sb", [P, 3, E])
        stats_b = sb("stats_b", [P, 3, 6])
        mv_b = sb("mv_b", [P, 3, 2])
        rstd_b = sb("rstd_b", [P, 3])
        stats_c = sb("stats_c", [P, 3, 6])
        mv_c = sb("mv_c", [P, 3, 2])
        rstd_c = sb("rstd_c", [P, 3])
        h2T = sb("h2T", [HALF, 2, S])
        gT = sb("gT", [P, HC, S])
        out_sb = sb("out_sb", [P, 3, E])

        score = [ctx.enter_context(nc.psum_tensor(f"score{r}", [P, 512], F32)) for r in range(RING)]
        work = [ctx.enter_context(nc.psum_tensor(f"work{r}", [P, 512], F32)) for r in range(NBANK)]

        alphas_in = sem("alphas_in")
        weights_in = sem("weights_in")
        pool_prep = sem("pool_prep")
        prep_step = sem("prep_step")
        x_in = sem("x_in")
        txt_in = sem("txt_in")
        score_full = [sem(f"score_full{r}") for r in range(RING)]
        score_free = [sem(f"score_free{r}") for r in range(RING)]
        work_full = [sem(f"work_full{r}") for r in range(NBANK)]
        work_free = [sem(f"work_free{r}") for r in range(NBANK)]
        max_ready = sem("max_ready")
        ln_ready = sem("ln_ready")
        log_ready = sem("log_ready")
        log_stacked = sem("log_stacked")
        parts_ready = sem("parts_ready")
        stacked = sem("stacked")
        var_ready = {s: sem(f"var_ready_{s}") for s in "fbc"}
        rstd_ready = {s: sem(f"rstd_ready_{s}") for s in "fbc"}
        hn_ready = sem("hn_ready")
        kappa_ready = sem("kappa_ready")
        v_ready = sem("v_ready")
        next_ready = sem("next_ready")
        cur_ready = sem("cur_ready")
        first_weights = sem("first_weights")
        half_weights = sem("half_weights")
        a_row_ready = sem("a_row_ready")
        v_weighted = sem("v_weighted")
        h2_ready = sem("h2_ready")
        h2n_ready = sem("h2n_ready")
        h2b_ready = sem("h2b_ready")
        out_stored = sem("out_stored")
        vector_step = {s: sem(f"vector_step_{s}") for s in LINKS}

        ROWS = (P, P, REST)
        WIDE = ((slice(0, 2), P), (slice(2, 3), REST))

        def spread(t, rows, n):
            return t[0:rows, :].unsqueeze(1).to_broadcast([rows, n, E])

        def wait(engine, semaphore, value):
            if not (isinstance(value, int) and value == 0):
                engine.wait_ge(semaphore, value)

        def wait_full(engine, p, job):
            engine.wait_ge(work_full[BANK[job]], p.uses_before(job) + 1)
            return work[BANK[job]]

        def wait_emptied(engine, p, *jobs):
            for job in {BANK[n]: n for n in sorted(jobs, key=JOBS.index)}.values():
                engine.wait_ge(work_free[BANK[job]], p.uses_before(job) + 1)

        def wait_exp(engine, image, slot):
            engine.wait_ge(score_free[slot % RING], image * RING_USES[slot % RING] + slot // RING + 1)

        def wait_scores(engine, image, slot):
            engine.wait_ge(score_full[slot % RING], image * RING_USES[slot % RING] + slot // RING + 1)

        OUT_FREE = 1
        WEIGHT_DMAS = 9 + 6 + 1 + 4
        POOL_PREPS = 27

        block = ctx.enter_context(nc.Block())

        @block.sync
        def _(sp):
            sp.dma_start(alpha_sb[:, 0:3], alpha_e.partition_broadcast(P)).then_inc(alphas_in, 16)
            sp.dma_start(alpha_sb[:, 3:6], alpha_r.partition_broadcast(P)).then_inc(alphas_in, 16)
            for dst, src in ((tok_w_sb, tok_w), (wq_sb, wq), (wk_sb, wk), (wv_sb, wv), (w0_sb, w_fc),
                             (w1_sb, w_proj), (bq_sb, bq), (bk_sb, bk), (b0_sb, b_fc)):
                sp.dma_start(dst[:], src).then_inc(weights_in, 16)
            for dst, src in ((tok_b_sb, tok_b), (bv_sb, bv), (bo_sb, bo), (ln_g_sb, ln_g),
                             (ln_b_sb, ln_b), (b1_sb, b_proj)):
                sp.dma_start(dst[:], src.partition_broadcast(P)).then_inc(weights_in, 16)
            sp.dma_start(h_sb[CLS_ROW:CLS_ROW + 1, 1, :], cls).then_inc(weights_in, 16)
            sp.wait_ge(pool_prep, 1)
            for j in range(4):
                sp.dma_start(wo_sb[32 * j:32 * j + D, :, :], wo[j]).then_inc(weights_in, 16)

            def store_logs(p, job, n, stack, row):
                wait_emptied(sp, p, job)
                sp.dma_start(stack[row:row + PARTS, :, 0:2 * P], log_rows[:]).then_inc(log_stacked, 16)
                sp.dma_start(stack[row:row + PARTS, :, 2 * P:SP], log_rest[:]).then_inc(log_stacked, 16)

            def one_pass(p):
                if p.front is not None:
                    if p.mid is not None:
                        sp.wait_ge(work_full[BANK["E_1"]], p.uses_last_pass("E_1"))
                    sp.dma_start(x_sb[:], x[p.front]).then_inc(x_in, 16)
                if p.mid is not None:
                    store_logs(p, "L", 0, q_stack[:, p.mid_parity], L_ROW)
                if p.front is not None:
                    if p.mid is not None:
                        sp.wait_ge(next_ready, 4 * p.mid + 4)
                    sp.dma_start(h_sb[CLS_ROW + 1:P, 1, :],
                                 txt[p.front, 0:P - CLS_ROW - 1, :]).then_inc(txt_in, 16)
                    sp.dma_start(h_sb[0:REST, 2, :],
                                 txt[p.front, P - CLS_ROW - 1:NTXT, :]).then_inc(txt_in, 16)
                if p.late is not None:
                    wait_emptied(sp, p, "O_2")
                    sp.dma_start(out[p.late, 0:2 * P, :].rearrange("(c p) e -> p c e", p=P),
                                 out_sb[:, 0:2, :]).then_inc(out_stored, 16)
                    sp.dma_start(out[p.late, 2 * P:S, :], out_sb[0:REST, 2, :]).then_inc(out_stored, 16)
                if p.mid is not None:
                    store_logs(p, "M", 1, k_stack[:, p.mid_parity], M_ROW)
                if p.front is not None:
                    if p.mid is None:
                        sp.wait_ge(prep_step, PREP_STEPS)
                    if p.back is not None:
                        wait_scores(sp, p.back, 3 * TILES - 1)
                    for t, (stack, blocks) in enumerate(((q_stack, Q_BLOCKS), (k_stack, K_BLOCKS))):
                        sp.wait_ge(parts_ready, 4 * p.front + 2 * t + 2)
                        for i, part in enumerate(blocks):
                            sp.dma_start(stack[D * i:D * i + D, p.front_parity, :, :],
                                         qk_parts[:, t, part, :, :]).then_inc(stacked, 16)

            run_passes(sp, B, one_pass)
            sp.wait_ge(out_stored, 32 * B + OUT_FREE)

        @block.gpsimd
        def _(pool):
            count = [0]

            def prep(ins):
                count[0] += 1
                ins.then_inc(pool_prep, 1)

            def after():
                pool.wait_ge(pool_prep, count[0])

            prep(pool.memset(wo_sb[:], 0.0))
            prep(pool.memset(ident[:], 0.0))
            prep(pool.memset(mask12[:], 1.0))
            prep(pool.memset(below[:], 1.0))
            prep(pool.memset(minus_half[:], -0.5))
            after()
            prep(pool.affine_select(out=ident[:], in_=ident[:], compare_op=ALU.not_equal, fill=1.0,
                                    base=0, pattern=[[-1, P]], channel_multiplier=1))
            prep(pool.affine_select(out=mask12[:, 8:12], in_=mask12[:, 8:12], compare_op=ALU.is_ge,
                                    fill=0.0, base=0, pattern=[[-32, 4]], channel_multiplier=1))
            after()
            prep(pool.affine_select(out=mask12[:, 8:12], in_=mask12[:, 8:12], compare_op=ALU.is_ge,
                                    fill=0.0, base=REST - 1, pattern=[[32, 4]], channel_multiplier=-1))
            for i, e in enumerate(EMBED_CHOICES):
                for j, r in enumerate(RATIO_CHOICES):
                    m = below[:, 3 * i + j, :]
                    prep(pool.affine_select(out=m, in_=m, compare_op=ALU.is_ge, fill=0.0,
                                            base=r * e - 1, pattern=[[-P, HC]], channel_multiplier=-1))
            for t in (hnT, qk_parts, v_w):
                prep(pool.memset(t[:], 0.0))
            for t in (sums, a_row, mv_f, mv_b, mv_c, hbo_next, hlb_next):
                prep(pool.memset(t[:], 1.0))
            assert count[0] == POOL_PREPS, count[0]

            def rstd(which, mv, out_, n):
                pool.wait_ge(var_ready[which], n + 1)
                nc.gpsimd.tensor_tensor(out_[:], mv[:, :, 1], minus_half[:], ALU.pow)\
                    .then_inc(rstd_ready[which], 1)

            def one_pass(p):
                if p.back is not None:
                    rstd("b", mv_b, rstd_b, p.back)
                    pool.wait_ge(h2_ready, p.back + 1)
                    if p.late is not None:
                        wait_emptied(pool, p, "O_2")
                    for c, rows in WIDE:
                        nc.gpsimd.tensor_tensor(h2b_sb[0:rows, c, :], h2_sb[0:rows, c, :],
                                                spread(b1_sb, rows, c.stop - c.start),
                                                ALU.add).then_inc(h2b_ready, 1)
                    rstd("c", mv_c, rstd_c, p.back)
                if p.front is not None:
                    rstd("f", mv_f, rstd_f, p.front)
                if p.mid is not None:
                    if p.back is not None:
                        pool.wait_ge(v_weighted, 3 * p.back + 3)
                    pool.wait_ge(v_ready, p.mid + 1)
                    pool.wait_ge(next_ready, 4 * p.mid + 4)
                    nc.gpsimd.tensor_tensor(pool_fence[:], pad_one[:], pad_one[:], ALU.add)
                    for dst, src in ((hbo_cur, hbo_next), (hlb_cur, hlb_next), (v_cur, v_sb)):
                        nc.gpsimd.tensor_copy(dst[:], src[:]).then_inc(cur_ready, 1)
                if p.front is not None:
                    pool.wait_ge(hn_ready, p.front + 1)
                    if p.mid is not None:
                        pool.wait_ge(cur_ready, 3 * p.mid + 3)
                    for dst, src, bias in ((hbo_next, hn_sb, bo_sb), (hlb_next, h_sb, ln_b_sb)):
                        for c, rows in WIDE:
                            nc.gpsimd.tensor_tensor(dst[0:rows, c, :], src[0:rows, c, :],
                                                    spread(bias, rows, c.stop - c.start),
                                                    ALU.add).then_inc(next_ready, 1)

            pool.wait_ge(weights_in, 16 * WEIGHT_DMAS)
            pool.wait_ge(prep_step, PREP_STEPS)
            run_passes(pool, B, one_pass)

        @block.tensor
        def _(pe):
            def work_bank(p, job, *inputs):
                wait(pe, work_free[BANK[job]], p.uses_before(job))
                wait_emptied(pe, p, *(n for n in inputs if BANK[n] != BANK[job]))
                return work[BANK[job]]

            def done(job, last):
                last.then_inc(work_full[BANK[job]], 1)

            def score_tiles(p, which, lo, hi):
                if p.mid is None:
                    return
                for k in range(lo, hi):
                    if k == 0 and which == 0:
                        pe.wait_ge(stacked, 16 * 2 * NBLK * (p.mid + 1))
                    elif k == 0:
                        pe.wait_ge(log_stacked, 32 * (2 * p.mid + which))
                    slot = TILES * which + k
                    r = slot % RING
                    wait(pe, score_free[r], p.mid * RING_USES[r] + slot // RING)
                    rows = (L_ROW, M_ROW, STACK)[which]
                    q_rows, k_rows = q_stack[0:rows, p.mid_parity], k_stack[0:rows, p.mid_parity]
                    still, move = (k_rows, q_rows) if which == 1 else (q_rows, k_rows)
                    g, h, c = tile_of(k)
                    if h is None:
                        for j in range(4):
                            last = nc.tensor.matmul(score[r][32 * j:32 * j + 32, 0:S],
                                                    still[:, 4 * g + j, 2 * P:SP],
                                                    move[:, 4 * g + j, 0:S], start=True, stop=True)
                    else:
                        last = nc.tensor.matmul(score[r][:, 0:S], still[:, h, P * c:P * c + P],
                                                move[:, h, 0:S], start=True, stop=True)
                    last.then_inc(score_full[r], 1)

            def four_heads(p, job, g, matrix, weights, *inputs):
                bank = work_bank(p, job, *inputs)
                for i in range(12):
                    c, j = divmod(i, 4)
                    k = 9 * g + (8 if c == 2 else 2 * j + c)
                    last = nc.tensor.matmul(bank[32 * j:32 * j + 32, 0:S], weights(i),
                                            matrix[:, k, :], start=(c == 0), stop=(c == 2))
                done(job, last)

            def half_sum(p, job, g, matrix, weights, *inputs):
                four_heads(p, job, g, matrix,
                           lambda i: weights[:, g, i:i + 1].to_broadcast([P, 32]), *inputs)

            def turn(p, job, g, rows, *inputs):
                bank = work_bank(p, job, *inputs)
                for c in range(2):
                    nc.tensor.transpose(bank[:, P * c:P * c + P], rows[:, g, P * c:P * c + P], ident[:])
                for j in range(4):
                    last = nc.tensor.matmul(bank[32 * j:32 * j + 32, 2 * P:3 * P:32],
                                            rows[:, g, 2 * P:SP], ident[:, 0:P:32], start=True, stop=True)
                done(job, last)

            def h4(p, g):
                if p.mid is not None:
                    pe.wait_ge(first_weights, 3 * p.mid + g + 1)
                    half_sum(p, f"H4_{g}", g, PL, w_a)

            def t4(p, g):
                if p.back is not None:
                    if BANK[f"H4_{g}"] != BANK[f"T4_{g}"]:
                        pe.wait_ge(work_free[BANK[f"H4_{g}"]], p.uses_last_pass(f"H4_{g}"))
                    turn(p, f"T4_{g}", g, sums)

            def h5(p, g):
                if p.back is not None:
                    pe.wait_ge(half_weights, 3 * p.back + g + 1)
                    half_sum(p, f"H5_{g}", g, G, w_b)

            def t5(p, g):
                if p.back is not None:
                    pe.wait_ge(a_row_ready, 3 * p.back + g + 1)
                    turn(p, f"T5_{g}", g, a_row)

            def h6(p, g):
                if p.back is not None:
                    half_sum(p, f"H6_{g}", g, PL, w_a2, f"T5_{g}")

            def t6(p, g):
                if p.back is not None:
                    turn(p, f"T6_{g}", g, sums, f"H6_{g}")

            def context(p, g):
                if p.back is not None:
                    pe.wait_ge(v_weighted, 3 * p.back + g + 1)
                    four_heads(p, f"C_{g}", g, G, lambda i: v_w[:, g, i, :])

            def turn_logs(p, job, n):
                if p.mid is None:
                    return
                pe.wait_ge(log_ready, 2 * p.mid + n + 1)
                bank = work_bank(p, job)[:, :].bitcast(BF16)
                n = PARTS * H
                nc.tensor.transpose(bank[0:PARTS * GROUPS, 2 * P:3 * P],
                                    log_parts[:, 2 * n:PARTS * TILES], ident_bf[:])
                for c in range(2):
                    last = nc.tensor.transpose(bank[0:n, P * c:P * c + P],
                                               log_parts[:, n * c:n * c + n], ident_bf[:])
                done(job, last)

            def out_proj(p, t):
                if p.back is None:
                    return
                job = f"W_{t}"
                bank = work_bank(p, job, *(f"C_{g}" for g in range(GROUPS)))
                for g in range(GROUPS):
                    last = nc.tensor.matmul(bank[0:ROWS[t], 0:E], ctxT[:, g, P * t:P * t + ROWS[t]],
                                            wo_sb[:, g, :], start=(g == 0), stop=(g == GROUPS - 1))
                done(job, last)

            def turn_tokens(p, job, half, src):
                bank = work_bank(p, job)
                for t in range(3):
                    last = nc.tensor.transpose(bank[0:HALF, P * t:P * t + ROWS[t]],
                                               src[0:ROWS[t], t, HALF * half:HALF * half + HALF],
                                               ident[0:ROWS[t], 0:ROWS[t]])
                done(job, last)

            def turn_h2(p, half):
                if p.back is not None:
                    pe.wait_ge(h2n_ready, p.back + 1)
                    turn_tokens(p, f"X_{half}", half, y_sb)

            def ffn_up(p, c):
                if p.late is None:
                    return
                job = f"G_{c}"
                bank = work_bank(p, job)
                for half in range(2):
                    if BANK[f"X_{half}"] != BANK[job]:
                        pe.wait_ge(work_free[BANK[f"X_{half}"]], p.uses_last_pass(f"X_{half}"))
                for half in range(2):
                    last = nc.tensor.matmul(bank[:, 0:S], w0_sb[:, half, P * c:P * c + P],
                                            h2T[:, half, :], start=(half == 0), stop=(half == 1))
                done(job, last)

            def ffn_down(p, t):
                if p.late is None:
                    return
                job = f"O_{t}"
                bank = work_bank(p, job, *(f"G_{c}" for c in range(HC)))
                for c in range(HC):
                    last = nc.tensor.matmul(bank[0:ROWS[t], 0:E], gT[:, c, P * t:P * t + ROWS[t]],
                                            w1_sb[:, c, :], start=(c == 0), stop=(c == HC - 1))
                done(job, last)

            def embed(p, t):
                if p.front is None:
                    return
                if t == 0:
                    pe.wait_ge(x_in, 16 * (p.front + 1))
                job = f"E_{t}"
                bank = work_bank(p, job)
                rows = (P, NPATCH - P)[t]
                for c in range(KC):
                    last = nc.tensor.matmul(bank[0:rows, 0:E], x_sb[:, c, P * t:P * t + rows],
                                            tok_w_sb[:, c, :], start=(c == 0), stop=(c == KC - 1))
                done(job, last)

            def turn_hn(p, half):
                if p.front is not None:
                    pe.wait_ge(hn_ready, p.front + 1)
                    turn_tokens(p, f"N_{half}", half, hn_sb)

            def project(p, name, m, w):
                if p.front is None:
                    return
                job = f"{name}_{m}"
                bank = work_bank(p, job, "N_0", "N_1")
                for half in range(2):
                    last = nc.tensor.matmul(bank[0:HALF, 0:S], w[:, half, m, :], hnT[:, half, 0:S],
                                            start=(half == 0), stop=(half == 1))
                done(job, last)

            def values(p, t):
                if p.front is None:
                    return
                job = f"V_{t}"
                bank = work_bank(p, job, "N_0", "N_1")
                for half in range(2):
                    if t < 2:
                        last = nc.tensor.matmul(bank[:, 0:E], hnT[:, half, P * t:P * t + P],
                                                wv_sb[:, half, :], start=(half == 0), stop=(half == 1))
                        continue
                    for j in range(4):
                        last = nc.tensor.matmul(bank[32 * j:32 * j + 32, 0:E], hnT[:, half, 2 * P:SP],
                                                wv_sb[:, half, :], start=(half == 0), stop=(half == 1))
                done(job, last)

            def one_pass(p):
                ffn_up(p, 0)
                ffn_up(p, 1)
                ffn_up(p, 2)
                ffn_up(p, 3)
                ffn_up(p, 4)
                ffn_up(p, 5)
                t4(p, 0)
                t4(p, 1)
                score_tiles(p, 0, 0, 4)
                h5(p, 0)
                score_tiles(p, 0, 4, 5)
                t4(p, 2)
                score_tiles(p, 0, 5, 8)
                h5(p, 1)
                score_tiles(p, 0, 8, 10)
                t5(p, 0)
                score_tiles(p, 0, 10, 12)
                h6(p, 0)
                score_tiles(p, 0, 12, 14)
                t5(p, 1)
                score_tiles(p, 0, 14, 16)
                h5(p, 2)
                score_tiles(p, 0, 16, 20)
                h6(p, 1)
                score_tiles(p, 0, 20, 21)
                t5(p, 2)
                score_tiles(p, 0, 21, 24)
                t6(p, 0)
                score_tiles(p, 0, 24, 25)
                t6(p, 1)
                score_tiles(p, 0, 25, TILES)
                h6(p, 2)
                context(p, 0)
                t6(p, 2)
                turn_logs(p, "L", 0)
                ffn_down(p, 0)
                ffn_down(p, 1)
                score_tiles(p, 1, 0, 4)
                context(p, 1)
                score_tiles(p, 1, 4, 8)
                context(p, 2)
                score_tiles(p, 1, 8, 13)
                out_proj(p, 0)
                score_tiles(p, 1, 13, 17)
                out_proj(p, 1)
                score_tiles(p, 1, 17, 21)
                out_proj(p, 2)
                score_tiles(p, 1, 21, TILES)
                ffn_down(p, 2)
                turn_logs(p, "M", 1)
                embed(p, 0)
                embed(p, 1)
                score_tiles(p, 2, 0, 9)
                turn_h2(p, 0)
                turn_h2(p, 1)
                score_tiles(p, 2, 9, 11)
                turn_hn(p, 0)
                score_tiles(p, 2, 11, 12)
                turn_hn(p, 1)
                score_tiles(p, 2, 12, 15)
                h4(p, 0)
                score_tiles(p, 2, 15, 17)
                project(p, "Q", 0, wq_sb)
                score_tiles(p, 2, 17, 19)
                values(p, 0)
                score_tiles(p, 2, 19, 21)
                project(p, "Q", 1, wq_sb)
                score_tiles(p, 2, 21, 24)
                project(p, "K", 0, wk_sb)
                score_tiles(p, 2, 24, 25)
                h4(p, 1)
                values(p, 1)
                score_tiles(p, 2, 25, TILES)
                project(p, "K", 1, wk_sb)
                values(p, 2)
                h4(p, 2)

            pe.wait_ge(prep_step, PREP_STEPS)
            run_passes(pe, B, one_pass)

        @block.scalar
        def _(act):
            def exp_tiles(p, which, lo, hi):
                if p.mid is None:
                    return
                for k in range(lo, hi):
                    slot = TILES * which + k
                    col = column_of(k)
                    if which < 2:
                        act.wait_ge(max_ready, 2 * TILES * p.mid + slot + 1)
                    else:
                        wait_scores(act, p.mid, slot)
                    neg, total, dst = ((neg_r, rho, junk[:, slot % RING, :]), (neg_c, kappa, G[:, k, :]),
                                       (None, sigma, PL[:, k, :]))[which]
                    bias = {} if neg is None else {"bias": neg[:, col:col + 1]}
                    nc.scalar.activation(dst, score[slot % RING][:, 0:S], ACT.Exp,
                                         accum_out=total[:, col:col + 1],
                                         **bias).then_inc(score_free[slot % RING], 1)

            def log_sums(p, n):
                if p.mid is not None:
                    wait_exp(act, p.mid, TILES * (n + 1) - 1)
                    nc.scalar.activation(ln_sum[:], (rho, kappa)[n][:], ACT.Ln).then_inc(ln_ready, 1)

            def a_rows(p, g):
                if p.back is None:
                    return
                job = f"H5_{g}"
                bank = wait_full(act, p, job)
                nc.scalar.activation(ln_row[:, g, :], bank[:, 0:S], ACT.Ln)\
                    .then_inc(work_free[BANK[job]], 1)
                wait_emptied(act, p, job)
                nc.scalar.activation(a_row[:, g, 0:S], ln_row[:, g, :], ACT.Exp, scale=-1.0)\
                    .then_inc(a_row_ready, 1)

            def copy_out(p, job, dst):
                if p.active(job):
                    bank = wait_full(act, p, job)
                    nc.scalar.activation(dst, bank[0:dst.shape[0], 0:S], ACT.Copy)\
                        .then_inc(work_free[BANK[job]], 1)

            def gelu(p, c):
                if p.late is None:
                    return
                job = f"G_{c}"
                bank = wait_full(act, p, job)
                nc.scalar.activation(gT[:, c, :], bank[:, 0:S], ACT.Gelu_apprx_tanh,
                                     bias=b0_sb[:, c:c + 1]).then_inc(work_free[BANK[job]], 1)
                if c == HC - 1:
                    act.preload_act_table_set("natural_log_exp_and_others")

            def one_pass(p):
                gelu(p, 0)
                gelu(p, 1)
                gelu(p, 2)
                gelu(p, 3)
                gelu(p, 4)
                gelu(p, 5)
                exp_tiles(p, 0, 0, 4)
                a_rows(p, 0)
                exp_tiles(p, 0, 4, 8)
                a_rows(p, 1)
                exp_tiles(p, 0, 8, 12)
                copy_out(p, "H6_0", sums[:, 0, 0:S])
                exp_tiles(p, 0, 12, 16)
                a_rows(p, 2)
                exp_tiles(p, 0, 16, 20)
                copy_out(p, "H6_1", sums[:, 1, 0:S])
                exp_tiles(p, 0, 20, TILES)
                log_sums(p, 0)
                copy_out(p, "H6_2", sums[:, 2, 0:S])
                exp_tiles(p, 1, 0, TILES)
                log_sums(p, 1)
                exp_tiles(p, 2, 0, 11)
                copy_out(p, "X_0", h2T[:, 0, :])
                copy_out(p, "N_0", hnT[:, 0, 0:S])
                exp_tiles(p, 2, 11, 12)
                copy_out(p, "X_1", h2T[:, 1, :])
                copy_out(p, "N_1", hnT[:, 1, 0:S])
                exp_tiles(p, 2, 12, 21)
                copy_out(p, "H4_0", sums[:, 0, 0:S])
                exp_tiles(p, 2, 21, TILES)
                copy_out(p, "H4_1", sums[:, 1, 0:S])
                copy_out(p, "H4_2", sums[:, 2, 0:S])

            act.preload_act_table_set("natural_log_exp_and_others")
            act.wait_ge(prep_step, PREP_STEPS)
            run_passes(act, B, one_pass)

        @block.vector
        def _(dve):
            count = [0]

            def prep(ins):
                count[0] += 1
                ins.then_inc(prep_step, 1)
                dve.wait_ge(prep_step, count[0])

            prep(nc.vector.memset(q_stack[L_ROW:STACK, :, :, :], 1.0))
            prep(nc.vector.memset(k_stack[L_ROW:STACK, :, :, :], 1.0))
            dve.wait_ge(pool_prep, POOL_PREPS)
            prep(nc.vector.tensor_copy(ident_bf[:], ident[:]))
            prep(nc.vector.reduce_sum(mask_rest[:], mask12[:, 8:12], AX_X))
            prep(nc.vector.tensor_scalar(pad_one[:], mask_rest[:], -1.0, 1.0, ALU.mult, ALU.add))
            prep(nc.vector.tensor_scalar(pad_neg[:], pad_one[:], NEG, None, ALU.mult))
            dve.wait_ge(alphas_in, 16 * 2)
            for i in range(3):
                prep(nc.vector.tensor_scalar(pair[:, 3 * i:3 * i + 3], alpha_sb[:, 3:6],
                                             alpha_sb[:, i:i + 1], None, ALU.mult))
            prep(nc.vector.memset(coef[:], 0.0))
            for i in (2, 1, 0):
                for j in range(3):
                    acc = coef[:, i + 1, :] if j == 0 and i < 2 else coef[:, i, :]
                    n = 3 * i + j
                    prep(nc.vector.scalar_tensor_tensor(out=coef[:, i, :], in0=below[:, n, :],
                                                        scalar=pair[:, n:n + 1], in1=acc,
                                                        op0=ALU.mult, op1=ALU.add))
            for i in range(3):
                prep(nc.vector.reduce_sum(coef_out[:, i:i + 1], pair[:, 3 * i:9], AX_X))
            coef_row = gT[0:HALF, :, :].rearrange("p c s -> p (c s)")[:, 0:2 * HID]\
                .rearrange("p (t h) -> p t h", t=2)
            prep(nc.vector.memset(coef_row, 0.0))
            for i, e in enumerate(EMBED_CHOICES):
                for j, r in enumerate(RATIO_CHOICES):
                    for half in range(2):
                        rows = min(max(e - HALF * half, 0), HALF)
                        if rows:
                            c = coef_row[0:rows, half, 0:r * e]
                            n = 3 * i + j
                            prep(nc.vector.tensor_scalar(c, c, pair[0:rows, n:n + 1], None, ALU.add))
            dve.wait_ge(weights_in, 16 * WEIGHT_DMAS)
            prep(nc.vector.tensor_tensor(b0_sb[:], b0_sb[:], coef[:, 0, :], ALU.mult))
            lo = 0
            for i, e in enumerate(EMBED_CHOICES):
                prep(nc.vector.tensor_tensor(w1_sb[:, :, lo:e], w1_sb[:, :, lo:e],
                                             coef[:, i, :].unsqueeze(2).to_broadcast([P, HC, e - lo]),
                                             ALU.mult))
                prep(nc.vector.tensor_scalar(b1_sb[:, lo:e], b1_sb[:, lo:e], coef_out[:, i:i + 1], None,
                                             ALU.mult))
                lo = e
            prep(nc.vector.tensor_tensor(w0_sb[:], w0_sb[:], coef_row, ALU.mult))
            assert count[0] == PREP_STEPS, count[0]

            nc.vector.memset(fence[:], 0.0).then_inc(out_stored, OUT_FREE)
            steps = {}

            def step(p, stage, ins):
                steps[stage] += 1
                ins.then_inc(vector_step[stage], 1)
                dve.wait_ge(vector_step[stage], p.images[stage] * LINKS[stage] + steps[stage])

            def max_tiles(p, which, lo, hi):
                if p.mid is None:
                    return
                for k in range(lo, hi):
                    slot = TILES * which + k
                    col = column_of(k)
                    wait_scores(dve, p.mid, slot)
                    nc.vector.tensor_reduce((neg_r, neg_c)[which][:, col:col + 1],
                                            score[slot % RING][:, 0:S], op=ALU.max, axis=AX_X,
                                            negate=True).then_inc(max_ready, 1)

            def logs(p, n):
                if p.mid is None:
                    return
                dve.wait_ge(ln_ready, 2 * p.mid + n + 1)
                step(p, "mid", nc.vector.tensor_tensor(log_f[:], (neg_r, neg_c)[n][:], ln_sum[:],
                                                       ALU.subtract))
                if n == 0:
                    f = log_f[:, 2 * H:TILES]
                    step(p, "mid", nc.vector.tensor_scalar(f, f, mask_rest[:], pad_neg[:],
                                                           ALU.mult, ALU.add))
                def whole(t):
                    return t[:, 0:2 * H].rearrange("p (c h) -> p c h", c=2)

                def rest(t):
                    return t[:, 2 * H:TILES]

                split_at = 2 * PARTS * H
                parts = [(log_parts[:, 0:split_at].rearrange("p (c n h) -> p c n h", c=2, n=PARTS)[:, :, i, :],
                          log_parts[:, split_at + GROUPS * i:split_at + GROUPS * i + GROUPS])
                         for i in range(PARTS)]
                both = (whole, rest)
                for i, view in enumerate(both):
                    last = nc.vector.tensor_copy(parts[0][i], view(log_f))
                step(p, "mid", last)
                for i, view in enumerate(both):
                    last = nc.vector.tensor_tensor(view(log_r), view(log_f), parts[0][i], ALU.subtract)
                step(p, "mid", last)
                for i, view in enumerate(both):
                    last = nc.vector.tensor_copy(parts[1][i], view(log_r))
                step(p, "mid", last)
                for i, view in enumerate(both):
                    last = nc.vector.tensor_tensor(parts[2][i], view(log_r), parts[1][i], ALU.subtract)
                last.then_inc(log_ready, 1)

            def log_rows_out(p, job, n):
                if p.mid is None:
                    return
                wait(dve, log_stacked, 32 * (2 * p.mid + n))
                bank = wait_full(dve, p, job)[:, :].bitcast(BF16)
                nc.vector.tensor_copy(log_rows[:], bank[0:PARTS * H, 0:2 * P])
                nc.vector.tensor_copy(log_rest[:], bank[0:PARTS * GROUPS, 2 * P:3 * P])\
                    .then_inc(work_free[BANK[job]], 1)

            def by_head(t, g):
                return t[:, 0:2 * H].rearrange("p (c h) -> p c h", c=2)[:, :, 4 * g:4 * g + 4]

            def kappa_weights(p):
                if p.mid is None:
                    return
                step(p, "mid", nc.vector.reciprocal(rest_tmp[:], kappa[:, 2 * H:TILES]))
                for g in range(GROUPS):
                    nc.vector.reciprocal(inv_kappa[:, g, 0:8].rearrange("p (c j) -> p c j", c=2),
                                         by_head(kappa, g))
                nc.vector.tensor_tensor(inv_kappa[:, :, 8:12],
                                        rest_tmp[:].unsqueeze(2).to_broadcast([P, GROUPS, 4]),
                                        mask12[:, 8:12].unsqueeze(1).to_broadcast([P, GROUPS, 4]),
                                        ALU.mult).then_inc(kappa_ready, 1)

            def first_half_weights(p, g):
                if p.mid is None:
                    return
                wait_exp(dve, p.mid, 2 * TILES + 9 * g + 8)
                nc.vector.reciprocal(w_a[:, g, 0:8].rearrange("p (c j) -> p c j", c=2),
                                     by_head(sigma, g))
                rest = sigma_rest[:, g:g + 1]
                step(p, "mid", nc.vector.tensor_scalar(rest, sigma[:, 2 * H + g:2 * H + g + 1],
                                                        pad_one[:], None, ALU.add))
                step(p, "mid", nc.vector.reciprocal(rest, rest))
                nc.vector.tensor_scalar(w_a[:, g, 8:12], mask12[:, 8:12], rest, None, ALU.mult)\
                    .then_inc(first_weights, 1)

            def turned(p, job):
                bank = wait_full(dve, p, job)
                return bank[:, 0:3 * P].rearrange("p (c j r) -> p c j r", c=3, r=32)[:, :, :, 0]

            def three(t, g):
                return t[:, g, :].rearrange("p (c j) -> p c j", c=3)

            def t4(p, g):
                if p.back is None:
                    return
                job = f"T4_{g}"
                nc.vector.reciprocal(three(recip12, g), turned(p, job)).then_inc(work_free[BANK[job]], 1)
                wait_emptied(dve, p, job)
                if g == 0:
                    dve.wait_ge(kappa_ready, p.back + 1)
                nc.vector.tensor_tensor(w_b[:, g, :], recip12[:, g, :], inv_kappa[:, g, :],
                                        ALU.mult).then_inc(half_weights, 1)

            def t5(p, g):
                if p.back is not None:
                    job = f"T5_{g}"
                    nc.vector.tensor_tensor(three(w_a2, g), turned(p, job),
                                            mask12[:].rearrange("p (c j) -> p c j", c=3),
                                            ALU.mult).then_inc(work_free[BANK[job]], 1)

            def t6(p, g):
                if p.back is None:
                    return
                job = f"T6_{g}"
                nc.vector.reciprocal(three(recip12, g), turned(p, job)).then_inc(work_free[BANK[job]], 1)
                wait_emptied(dve, p, job)
                step(p, "back", nc.vector.tensor_tensor(w_b2[:, g, :], recip12[:, g, :],
                                                        inv_kappa[:, g, :], ALU.mult))
                if g == 0:
                    dve.wait_ge(cur_ready, 3 * p.back + 3)
                heads = v_cur[:, :, 4 * D * g:4 * D * g + 4 * D]
                nc.vector.tensor_tensor(
                    v_w[:, g, :, 0:D].rearrange("p (c j) d -> p c j d", c=3),
                    heads.rearrange("p c (j d) -> p c j d", j=4),
                    three(w_b2, g).unsqueeze(3).to_broadcast([P, 3, 4, D]),
                    ALU.mult).then_inc(v_weighted, 1)

            def context(p, g):
                if p.back is None:
                    return
                job = f"C_{g}"
                dve.wait_ge(a_row_ready, 3 * p.back + g + 1)
                bank = wait_full(dve, p, job)
                nc.vector.tensor_tensor(ctxT[:, g, :], bank[:, 0:S], a_row[:, g, 0:S], ALU.mult)\
                    .then_inc(work_free[BANK[job]], 1)

            def statistics(p, stage, src, stats, mv, eps, ready):
                for t in range(3):
                    last = nc.vector.bn_stats(stats[0:ROWS[t], t, :], src[0:ROWS[t], t, :])
                step(p, stage, last)
                nc.vector.memset(fence[:], 0.0)
                for t in range(3):
                    last = nc.vector.bn_aggr(mv[0:ROWS[t], t, :], stats[0:ROWS[t], t, :])
                step(p, stage, last)
                nc.vector.tensor_scalar(mv[:, :, 1], mv[:, :, 1], eps, None, ALU.add)\
                    .then_inc(ready, 1)

            def output_tokens(p, t):
                if p.back is None:
                    return
                job = f"W_{t}"
                bank = wait_full(dve, p, job)
                rows = ROWS[t]
                nc.vector.tensor_tensor(y_sb[0:rows, t, :], bank[0:rows, 0:E],
                                        hbo_cur[0:rows, t, :], ALU.add)\
                    .then_inc(work_free[BANK[job]], 1)

            def output_statistics(p):
                if p.back is not None:
                    wait_emptied(dve, p, "W_0", "W_1", "W_2")
                    statistics(p, "back", y_sb, stats_b, mv_b, ATTN_EPS, var_ready["b"])

            def residual(p):
                if p.back is None:
                    return
                dve.wait_ge(rstd_ready["b"], p.back + 1)
                for t in range(3):
                    rows = ROWS[t]
                    last = nc.vector.scalar_tensor_tensor(
                        out=y_sb[0:rows, t, :], in0=y_sb[0:rows, t, :], scalar=mv_b[0:rows, t, 0:1],
                        in1=ln_g_sb[0:rows, :], op0=ALU.subtract, op1=ALU.mult)
                step(p, "back", last)

            def residual_add(p):
                if p.back is None:
                    return
                for t in range(3):
                    rows = ROWS[t]
                    last = nc.vector.scalar_tensor_tensor(
                        out=h2_sb[0:rows, t, :], in0=y_sb[0:rows, t, :], scalar=rstd_b[0:rows, t:t + 1],
                        in1=hlb_cur[0:rows, t, :], op0=ALU.mult, op1=ALU.add)
                last.then_inc(h2_ready, 1)

            def residual_statistics(p):
                if p.back is not None:
                    dve.wait_ge(h2_ready, p.back + 1)
                    statistics(p, "back", h2_sb, stats_c, mv_c, LN_EPS, var_ready["c"])

            def normalise(p, image, src, dst, mv, rstd, which, ready):
                dve.wait_ge(rstd_ready[which], image + 1)
                for t in range(3):
                    rows = ROWS[t]
                    last = nc.vector.tensor_scalar(dst[0:rows, t, :], src[0:rows, t, :],
                                                   mv[0:rows, t, 0:1], rstd[0:rows, t:t + 1],
                                                   ALU.subtract, ALU.mult)
                last.then_inc(ready, 1)

            def ffn_out(p, t):
                if p.late is None:
                    return
                job = f"O_{t}"
                if t == 0:
                    dve.wait_ge(h2b_ready, 2 * p.late + 2)
                    dve.wait_ge(out_stored, 32 * p.late + OUT_FREE)
                bank = wait_full(dve, p, job)
                rows = ROWS[t]
                nc.vector.tensor_tensor(out_sb[0:rows, t, :], bank[0:rows, 0:E], h2b_sb[0:rows, t, :],
                                        ALU.add).then_inc(work_free[BANK[job]], 1)

            def embed(p, t):
                if p.front is None:
                    return
                if t == 0 and p.mid is not None:
                    dve.wait_ge(next_ready, 4 * p.mid + 4)
                job = f"E_{t}"
                bank = wait_full(dve, p, job)
                rows = (P, NPATCH - P)[t]
                nc.vector.tensor_tensor(h_sb[0:rows, t, :], bank[0:rows, 0:E], tok_b_sb[0:rows, :],
                                        ALU.add).then_inc(work_free[BANK[job]], 1)

            def embed_statistics(p):
                if p.front is None:
                    return
                wait_emptied(dve, p, "E_0", "E_1")
                dve.wait_ge(txt_in, 32 * (p.front + 1))
                statistics(p, "front", h_sb, stats_f, mv_f, LN_EPS, var_ready["f"])

            def take_qk(p, name, m, bias, scale):
                if p.front is not None:
                    job = f"{name}_{m}"
                    bank = wait_full(dve, p, job)
                    nc.vector.tensor_scalar(qk_f[:, 2 * (name == "K") + m, 0:S], bank[0:HALF, 0:S],
                                            bias[:, m:m + 1], scale, ALU.add, ALU.mult)\
                        .then_inc(work_free[BANK[job]], 1)

            def split_qk(p, name, m):
                if p.front is None:
                    return
                i = 2 * (name == "K") + m
                wait_emptied(dve, p, f"{name}_{m}")
                if i == 0:
                    wait(dve, stacked, 16 * 2 * NBLK * p.front)
                part = [qk_parts[:, i // 2, n, m, 0:S] for n in range(PARTS)]
                step(p, "front", nc.vector.tensor_copy(part[0], qk_f[:, i, 0:S]))
                step(p, "front", nc.vector.tensor_tensor(qk_r[:, 0:S], qk_f[:, i, 0:S], part[0],
                                                         ALU.subtract))
                step(p, "front", nc.vector.tensor_copy(part[1], qk_r[:, 0:S]))
                nc.vector.tensor_tensor(part[2], qk_r[:, 0:S], part[1], ALU.subtract)\
                    .then_inc(parts_ready, 1)

            def values(p, t):
                if p.front is None:
                    return
                if t == 0 and p.mid is not None:
                    dve.wait_ge(cur_ready, 3 * p.mid + 3)
                job = f"V_{t}"
                bank = wait_full(dve, p, job)
                nc.vector.tensor_tensor(v_sb[:, t, :], bank[:, 0:E], bv_sb[:], ALU.add)\
                    .then_inc(work_free[BANK[job]], 1)
                if t == 2:
                    wait_emptied(dve, p, "V_0", "V_1", "V_2")
                    nc.vector.memset(fence[:], 0.0).then_inc(v_ready, 1)

            def one_pass(p):
                steps.update(dict.fromkeys(LINKS, 0))
                t4(p, 0)
                max_tiles(p, 0, 0, 1)
                t4(p, 1)
                max_tiles(p, 0, 1, 8)
                t5(p, 0)
                max_tiles(p, 0, 8, 11)
                t4(p, 2)
                max_tiles(p, 0, 11, 13)
                t5(p, 1)
                max_tiles(p, 0, 13, 21)
                t5(p, 2)
                max_tiles(p, 0, 21, TILES)
                t6(p, 0)
                t6(p, 1)
                logs(p, 0)
                context(p, 0)
                log_rows_out(p, "L", 0)
                t6(p, 2)
                max_tiles(p, 1, 0, 4)
                ffn_out(p, 0)
                max_tiles(p, 1, 4, 5)
                context(p, 1)
                ffn_out(p, 1)
                max_tiles(p, 1, 5, 10)
                context(p, 2)
                max_tiles(p, 1, 10, 17)
                output_tokens(p, 0)
                max_tiles(p, 1, 17, 21)
                output_tokens(p, 1)
                max_tiles(p, 1, 21, 24)
                output_tokens(p, 2)
                max_tiles(p, 1, 24, TILES)
                output_statistics(p)
                logs(p, 1)
                ffn_out(p, 2)
                residual(p)
                log_rows_out(p, "M", 1)
                residual_add(p)
                embed(p, 0)
                residual_statistics(p)
                embed(p, 1)
                embed_statistics(p)
                if p.back is not None:
                    normalise(p, p.back, h2_sb, y_sb, mv_c, rstd_c, "c", h2n_ready)
                if p.front is not None:
                    normalise(p, p.front, h_sb, hn_sb, mv_f, rstd_f, "f", hn_ready)
                kappa_weights(p)
                first_half_weights(p, 0)
                take_qk(p, "Q", 0, bq_sb, D ** -0.5)
                split_qk(p, "Q", 0)
                take_qk(p, "Q", 1, bq_sb, D ** -0.5)
                first_half_weights(p, 1)
                values(p, 0)
                split_qk(p, "Q", 1)
                take_qk(p, "K", 0, bk_sb, 1.0)
                split_qk(p, "K", 0)
                first_half_weights(p, 2)
                take_qk(p, "K", 1, bk_sb, 1.0)
                values(p, 1)
                split_qk(p, "K", 1)
                values(p, 2)
                for stage, n in steps.items():
                    assert p.images[stage] is None or n == LINKS[stage], (stage, n)

            run_passes(dve, B, one_pass)


def lay_out(inputs):
    import numpy as np

    a = {k: np.asarray(v) for k, v in inputs.items()}
    B = a["x"].shape[0]
    x = a["x"].reshape(B, 3, 14, 16, 14, 16).transpose(0, 1, 3, 5, 2, 4).reshape(B, KC, P, NPATCH)

    def halves(w):
        return w.reshape(2, HALF, -1).transpose(1, 0, 2)

    def qk(w):
        w = w.reshape(2, HALF, HH, 2, D).transpose(1, 0, 3, 4, 2)
        return w.reshape(HALF, 2, 2, HALF)

    def qk_bias(b):
        return b.reshape(HH, 2, D).transpose(2, 0, 1).reshape(HALF, 2)

    d = {
        "x": x.transpose(0, 2, 1, 3),
        "txt": a["txt"],
        "tok_w": a["L0_tok_W"].reshape(KC, P, E).transpose(1, 0, 2),
        "tok_b": a["L0_tok_b"],
        "cls": a["L0_tok_cls_token"].reshape(1, E),
        "wq": qk(a["L0_attn_Wq"]), "wk": qk(a["L0_attn_Wk"]), "wv": halves(a["L0_attn_Wv"]),
        "wo": a["L0_attn_Wo"].reshape(GROUPS, 4, D, E).transpose(1, 2, 0, 3),
        "bq": qk_bias(a["L0_attn_bq"]), "bk": qk_bias(a["L0_attn_bk"]),
        "bv": a["L0_attn_bv"], "bo": a["L0_attn_bo"],
        "ln_g": a["L0_attn_ln_g"], "ln_b": a["L0_attn_ln_b"],
        "w_fc": halves(a["L0_ffn_w_fc"].T),
        "b_fc": a["L0_ffn_b_fc"].reshape(HC, P).T,
        "w_proj": a["L0_ffn_w_proj"].T.reshape(HC, P, E).transpose(1, 0, 2),
        "b_proj": a["L0_ffn_b_proj"],
        "alpha_e": a["L0_ffn_alpha_e"], "alpha_r": a["L0_ffn_alpha_r"],
    }
    return {k: np.ascontiguousarray(v) for k, v in d.items()}


def kernel(**inputs):
    import numpy as np
    import concourse.bacc as bacc
    from concourse.bass_utils import run_bass_kernel_spmd

    nc = bacc.Bacc("TRN2", target_bir_lowering=False, num_devices=1)
    arrays = {f"in_{k}": v for k, v in lay_out(inputs).items()}
    args = {k[3:]: nc.dram_tensor(k, v.shape, mybir.dt.from_np(v.dtype), kind="ExternalInput").ap()
            for k, v in arrays.items()}
    B = arrays["in_x"].shape[0]
    out = nc.dram_tensor("out_tokens", (B, S, E), F32, kind="ExternalOutput").ap()
    early_fusion_kernel(nc, out=out, **args)
    got = np.asarray(run_bass_kernel_spmd(nc, [arrays], core_ids=[0]).results[0]["out_tokens"])
    return np.concatenate([got[:, NPATCH:NPATCH + 1], got[:, :NPATCH], got[:, NPATCH + 1:]], axis=1)
```
